# Optimizing a Trainium2 kernel written in Bass

```python
import numpy as np
import jax
import jax.numpy as jnp

def _softmax(x, axis=-1):
    return jax.nn.softmax(x, axis=axis)

def _gelu(x):
    return jax.nn.gelu(x, approximate=True)

def _silu(x):
    return jax.nn.silu(x)

def _sigmoid(x):
    return jax.nn.sigmoid(x)

def _layernorm(x, axis=-1, eps=1e-05):
    m = jnp.mean(x, axis=axis, keepdims=True)
    v = jnp.var(x, axis=axis, keepdims=True)
    return (x - m) / jnp.sqrt(v + eps)

def _scatter_add(tgt, idx, src, axis=0):
    return tgt.at[idx].add(src)

def _segment_sum(src, seg, n):
    return jax.ops.segment_sum(src, seg, n)
kernel_name = 'mk_seq_postln_d1_jaxref_r8_73e5c8'

def setup_inputs(seed: int=0):
    np.random.seed(seed)
    _w = jnp.asarray

    def _L0_attn_setup():
        import jax, jax.numpy as jnp
        import numpy as np
        B, S, D = (1, 256, 256)
        KV_RANK, Q_RANK = (64, 192)
        H, HKV = (16, 16)
        DR, DN, DV = (64, 128, 128)
        THETA = 10000.0

        def _rope_tables(seq_len, dim):
            inv_freq = 1.0 / THETA ** (jnp.arange(0, dim, 2, dtype=jnp.float32) / dim)
            ang = jnp.arange(seq_len, dtype=jnp.float32)[:, None] * inv_freq[None, :]
            return (jnp.cos(ang), jnp.sin(ang))

        def _apply_rope(t, cos, sin):
            te, to = (t[..., 0::2], t[..., 1::2])
            c, s = (cos[None, :, None, :], sin[None, :, None, :])
            re = te * c - to * s
            ro = te * s + to * c
            return jnp.stack([re, ro], axis=-1).reshape(t.shape)
        key = jax.random.key(seed)
        ks = jax.random.split(key, 9)
        w = lambda k, i, o: jax.random.normal(k, (i, o), jnp.float32) * 0.02
        return {'x': jax.random.normal(ks[0], (B, S, D), jnp.float32), 'w_dkv': w(ks[1], D, KV_RANK), 'w_kr': w(ks[2], D, DR), 'w_uk': w(ks[3], KV_RANK, HKV * DN), 'w_uv': w(ks[4], KV_RANK, HKV * DV), 'w_dq': w(ks[5], D, Q_RANK), 'w_qr': w(ks[6], Q_RANK, H * DR), 'w_uq': w(ks[7], Q_RANK, H * DN), 'w_o': w(ks[8], H * DV, D)}
    _L0_attn_in = _L0_attn_setup()

    def _L0_ffn_setup():
        import jax, jax.numpy as jnp
        import numpy as np
        D_MODEL = 256
        HIDDEN = int(2 * D_MODEL * 4 / 3)

        def ternary_quant(w):
            s = jnp.mean(jnp.abs(w))
            q = jnp.clip(jnp.round(w / s), -1.0, 1.0) * s
            return w + jax.lax.stop_gradient(q - w)
        key = jax.random.key(seed)
        k0, k1, k2, k3 = jax.random.split(key, 4)
        x = jax.random.normal(k0, (4, 512, D_MODEL), dtype=jnp.float32)
        std_in = 1.0 / np.sqrt(D_MODEL)
        std_h = 1.0 / np.sqrt(HIDDEN)
        w1 = jax.random.uniform(k1, (HIDDEN, D_MODEL), jnp.float32, -std_in, std_in)
        w3 = jax.random.uniform(k2, (HIDDEN, D_MODEL), jnp.float32, -std_in, std_in)
        w2 = jax.random.uniform(k3, (D_MODEL, HIDDEN), jnp.float32, -std_h, std_h)
        return {'x': x, 'w1': w1, 'w3': w3, 'w2': w2}
    _L0_ffn_in = _L0_ffn_setup()
    _d = {'L0_attn_x': _L0_attn_in['x'], 'L0_attn_w_dkv': _L0_attn_in['w_dkv'], 'L0_attn_w_kr': _L0_attn_in['w_kr'], 'L0_attn_w_uk': _L0_attn_in['w_uk'], 'L0_attn_w_uv': _L0_attn_in['w_uv'], 'L0_attn_w_dq': _L0_attn_in['w_dq'], 'L0_attn_w_qr': _L0_attn_in['w_qr'], 'L0_attn_w_uq': _L0_attn_in['w_uq'], 'L0_attn_w_o': _L0_attn_in['w_o'], 'L0_ffn_w1': _L0_ffn_in['w1'], 'L0_ffn_w3': _L0_ffn_in['w3'], 'L0_ffn_w2': _L0_ffn_in['w2']}
    _x0 = _d['L0_attn_x']
    _d['L0_attn_x'] = jax.random.normal(jax.random.fold_in(jax.random.key(seed), 1), (2, 1024, 256), dtype=_x0.dtype)
    del _x0
    return _d

def reference(L0_attn_x, L0_attn_w_dkv, L0_attn_w_kr, L0_attn_w_uk, L0_attn_w_uv, L0_attn_w_dq, L0_attn_w_qr, L0_attn_w_uq, L0_attn_w_o, L0_ffn_w1, L0_ffn_w3, L0_ffn_w2):

    def _L0_attn_ref(x, w_dkv, w_kr, w_uk, w_uv, w_dq, w_qr, w_uq, w_o):
        import jax, jax.numpy as jnp
        import numpy as np
        B, S, D = (1, 256, 256)
        KV_RANK, Q_RANK = (64, 192)
        H, HKV = (16, 16)
        DR, DN, DV = (64, 128, 128)
        THETA = 10000.0

        def _rope_tables(seq_len, dim):
            inv_freq = 1.0 / THETA ** (jnp.arange(0, dim, 2, dtype=jnp.float32) / dim)
            ang = jnp.arange(seq_len, dtype=jnp.float32)[:, None] * inv_freq[None, :]
            return (jnp.cos(ang), jnp.sin(ang))

        def _apply_rope(t, cos, sin):
            te, to = (t[..., 0::2], t[..., 1::2])
            c, s = (cos[None, :, None, :], sin[None, :, None, :])
            re = te * c - to * s
            ro = te * s + to * c
            return jnp.stack([re, ro], axis=-1).reshape(t.shape)
        b, s, d = x.shape
        cos, sin = _rope_tables(s, DR)
        c_kv = x @ w_dkv
        c_q = x @ w_dq
        k_r = _apply_rope((x @ w_kr).reshape(b, s, 1, DR), cos, sin)
        k_r = jnp.broadcast_to(k_r, (b, s, HKV, DR))
        k_n = (c_kv @ w_uk).reshape(b, s, HKV, DN)
        k = jnp.concatenate([k_r, k_n], axis=-1)
        q_r = _apply_rope((c_q @ w_qr).reshape(b, s, H, DR), cos, sin)
        q_n = (c_q @ w_uq).reshape(b, s, H, DN)
        q = jnp.concatenate([q_r, q_n], axis=-1)
        v = (c_kv @ w_uv).reshape(b, s, HKV, DV)
        scale = 1.0 / jnp.sqrt(jnp.float32(DR + DN))
        scores = jnp.einsum('bqhd,bkhd->bhqk', q, k) * scale
        attn = jax.nn.softmax(scores, axis=-1)
        out = jnp.einsum('bhqk,bkhd->bqhd', attn, v)
        out = out.reshape(b, s, H * DV)
        return out @ w_o

    def _L0_ffn_ref(x, w1, w3, w2):
        import jax, jax.numpy as jnp
        import numpy as np
        D_MODEL = 256
        HIDDEN = int(2 * D_MODEL * 4 / 3)

        def ternary_quant(w):
            s = jnp.mean(jnp.abs(w))
            q = jnp.clip(jnp.round(w / s), -1.0, 1.0) * s
            return w + jax.lax.stop_gradient(q - w)
        w1q = ternary_quant(w1)
        w3q = ternary_quant(w3)
        w2q = ternary_quant(w2)
        h1 = jnp.einsum('bsd,hd->bsh', x, w1q)
        h3 = jnp.einsum('bsd,hd->bsh', x, w3q)
        g = jax.nn.silu(h1) * h3
        return jnp.einsum('bsh,dh->bsd', g, w2q)
    x = L0_attn_x
    x = _layernorm(x + _L0_attn_ref(x, L0_attn_w_dkv, L0_attn_w_kr, L0_attn_w_uk, L0_attn_w_uv, L0_attn_w_dq, L0_attn_w_qr, L0_attn_w_uq, L0_attn_w_o), axis=-1)
    x = _layernorm(x + _L0_ffn_ref(x, L0_ffn_w1, L0_ffn_w3, L0_ffn_w2), axis=-1)
    return x

_drawn_inputs = setup_inputs


def setup_inputs(seed=0):
    import zlib

    import numpy as np

    out = dict(_drawn_inputs(seed))
    spreads = {}
    factors = {'L0_attn_w_dkv': 8.0,
     'L0_attn_w_kr': 8.0,
     'L0_attn_w_uk': 8.0,
     'L0_attn_w_uv': 8.0,
     'L0_attn_w_dq': 8.0,
     'L0_attn_w_qr': 8.0,
     'L0_attn_w_uq': 8.0,
     'L0_attn_w_o': 8.0}
    for name, (base, spread) in spreads.items():
        noise = np.random.default_rng([zlib.crc32(name.encode()), seed]).standard_normal(out[name].shape)
        drawn = base * np.exp(spread * noise) if base else spread * noise
        out[name] = jnp.asarray(drawn.astype(out[name].dtype))
    for name, factor in factors.items():
        out[name] = (out[name] * factor).astype(out[name].dtype)
    return out
```

```python
import math
from contextlib import ExitStack

import numpy as np

import concourse.bass as bass
from concourse import mybir

B, S, D = 2, 1024, 256
H, DR, DN, DV = 16, 64, 128, 128
KVR, QR = 64, 192
HID = 682
THETA = 10000.0
EPS = 1e-5
P = 128
QT = S // P
KT = S // P
KC = D // P
PAIRS = H // 2
HALF = S // 2
GROUPS = 4
HT = -(-HID // P)
LAST = HID - (HT - 1) * P
W = 3 * HT * D
PROB_UP = 2.0 ** 14
VAL_UP = 2.0 ** 8
TILES = 4 * 4

EXP0, PT0, LO0, OUT0, ROW0 = 2, 4, 2, 1, 1


def rope_tables():
    inv = np.float32(1.0) / np.float32(THETA) ** (np.arange(0, DR, 2, dtype=np.float32) / np.float32(DR))
    ang = np.arange(S, dtype=np.float32)[:, None] * inv[None, :].astype(np.float32)
    cos = np.cos(ang.astype(np.float64)).astype(np.float32).T
    sin = np.sin(ang.astype(np.float64)).astype(np.float32).T
    return np.ascontiguousarray(np.tile(cos, (4, 1))), np.ascontiguousarray(np.tile(sin, (4, 1)))


def build(nc, x, w_dkv, w_kr, w_uk, w_uv, w_dq, w_qr, w_uq, w_o, w1, w3, w2, cos, sin, out):
    F = mybir.dt.float32
    R = mybir.dt.float32r
    F16 = mybir.dt.float16
    I32 = mybir.dt.int32
    ALU = mybir.AluOpType
    ACT = mybir.ActivationFunctionType
    AX = mybir.AxisListType
    SCALE = 1.0 / math.sqrt(DR + DN)

    x_v = x.rearrange("b (t p) d -> b p t d", p=P)
    out_v = out.rearrange("b (t p) d -> b p t d", p=P)
    wo_v = w_o.rearrange("(h n) d -> n h d", n=DV)
    ternary = nc.dram_tensor("ternary", [P, W], F, kind="Internal").ap()

    ctx = ExitStack()
    with ctx:
        def sem(name):
            return ctx.enter_context(nc.semaphore(name))

        def sb(stack, name, shape, dt):
            return stack.enter_context(nc.sbuf_tensor(name, shape, dt))

        ident = sb(ctx, "ident", [P, P], F)
        ones = sb(ctx, "ones", [P, P], F)
        Wq_hi = sb(ctx, "Wq_hi", [P, H, 2, P], R)
        Wq_lo = sb(ctx, "Wq_lo", [P, H, 2, P], R)
        Wvo = sb(ctx, "Wvo", [P, PAIRS, D], F)
        K_hi = sb(ctx, "K_hi", [P, S], R)
        K_lo = sb(ctx, "K_lo", [P, S], R)
        V_hi = sb(ctx, "V_hi", [P, KT, KVR], F16)
        V_lo = sb(ctx, "V_lo", [P, KT, KVR], F16)
        vscale = sb(ctx, "vscale", [P, 4], F)
        ffs = sb(ctx, "ffs", [P, 8], F)
        minus_half = sb(ctx, "minus_half", [P, 4], F)

        with ExitStack() as st:
            wuq_a = sb(st, "wuq_a", [P, H * DN], F)
            wuq_b = sb(st, "wuq_b", [QR - P, H * DN], F)
            wuk = sb(st, "wuk", [KVR, H * DN], F)
            wuv = sb(st, "wuv", [KVR, H * DV], F)
            wo = sb(st, "wo", [P, H, D], F)
            wqr = sb(st, "wqr", [P, 2, H * DR], F)
            wT = sb(st, "wT", [P, 2, 384], F)
            w13 = sb(st, "w13", [P, 2, HT, D], F)
            w2n = sb(st, "w2n", [P, KC, HT * P], F)
            below = sb(st, "below", [P, HT * D], F)
            asum = sb(st, "asum", [P, 4], F)
            tern = sb(st, "tern", [P, W], R)

        QO = sb(ctx, "QO", [P, H, S], F)

        with ExitStack() as st:
            xq = sb(st, "xq", [P, QT, D], F)
            tcos = sb(st, "tcos", [P, S], F)
            tsin = sb(st, "tsin", [P, S], F)
            wkv_raw = sb(st, "wkv_raw", [P, KC, P], F)
            wkv = sb(st, "wkv", [P, KC, P], F)
            wdq = sb(st, "wdq", [P, KC, QR], F)
            wdq_b = sb(st, "wdq_b", [P, KC, 2, QR - P], F)
            xT = sb(st, "xT", [P, KC, S], F)
            Kf = sb(st, "Kf", [P, S], F)
            kmul = sb(st, "kmul", [P, 2, S], F)
            cq_hi = sb(st, "cq_hi", [P, S], R)
            cq_lo = sb(st, "cq_lo", [P, S], R)
            cq_s = sb(st, "cq_s", [P, S], R)
            qmul = sb(st, "qmul", [P, 4, S], F)
            turned = sb(st, "turned", [P, 2, 2, S], F)

        with ExitStack() as st:
            Q_hi = sb(st, "Q_hi", [P, 2, S], R)
            Q_lo = sb(st, "Q_lo", [P, 2, S], R)
            probs = sb(st, "probs", [P, 2, S], F)
            PT_hi = sb(st, "PT_hi", [P, 2, 2, KT, HALF], F16)
            PT_lo = sb(st, "PT_lo", [P, 2, 2, KT, HALF], F16)
            nmax = sb(st, "nmax", [P, 4], F)
            den = sb(st, "den", [P, 2, 2, 4], F)
            rden = sb(st, "rden", [P, 2, 2, 4], F)
            rden_wide = sb(st, "rden_wide", [P, 4, 2, KVR], F)
            rden_row = sb(st, "rden_row", [P, HALF], F)

        with ExitStack() as st:
            xr = sb(st, "xr", [P, QT, D], F)
            TT = sb(st, "TT", [P, W], R)
            res = sb(st, "res", [P, QT, D], F)
            x1 = sb(st, "x1", [P, QT, D], F)
            yo = sb(st, "yo", [P, 4, D], F)
            x1T_hi = sb(st, "x1T_hi", [P, KC, HALF], R)
            x1T_lo = sb(st, "x1T_lo", [P, KC, HALF], R)
            act = sb(st, "act", [P, 2, HALF], F)
            gate = sb(st, "gate", [P, 2, HALF], F)
            g_hi = sb(st, "g_hi", [P, HT, HALF], R)
            g_lo = sb(st, "g_lo", [P, HT, HALF], R)
            stats = sb(st, "stats", [P, QT, 6], F)
            mv = sb(st, "mv", [P, QT, 2], F)
            ve = sb(st, "ve", [P, QT], F)
            rstd = sb(st, "rstd", [P, QT], F)

        Sa = ctx.enter_context(nc.psum_tensor("Sa", [P, S], F))
        Sb = ctx.enter_context(nc.psum_tensor("Sb", [P, S], F))
        Ta = ctx.enter_context(nc.psum_tensor("Ta", [P, HALF], F))
        Tb = ctx.enter_context(nc.psum_tensor("Tb", [P, HALF], F))
        Oa = ctx.enter_context(nc.psum_tensor("Oa", [P, HALF], F))
        Ob = ctx.enter_context(nc.psum_tensor("Ob", [P, HALF], F))
        SS, TS, OS = (Sa, Sb), (Ta, Tb), (Oa, Ob)

        phase = sem("phase")
        held = sem("held")
        const_ready = sem("const_ready")
        w_qk_in, w_o_in, w_qr_in, w_ff_in = sem("w_qk_in"), sem("w_o_in"), sem("w_qr_in"), sem("w_ff_in")
        pad_ready = sem("pad_ready")
        wt_ps, wt_sb = sem("wt_ps"), sem("wt_sb")
        prod_ps, prod_hi, prod_lo = sem("prod_ps"), sem("prod_hi"), sem("prod_lo")
        qr_hi = sem("qr_hi")
        ff_sum, ff_mean, ff_step = sem("ff_sum"), sem("ff_mean"), sem("ff_step")
        ff_tern, ff_ps, ff_sb, ff_out = sem("ff_tern"), sem("ff_ps"), sem("ff_sb"), sem("ff_out")
        proj_in = sem("proj_in")
        w_small = sem("w_small")
        xT_ps, xT_sb = sem("xT_ps"), sem("xT_sb")
        kv_ps, cqa_ps, cqb_ps = sem("kv_ps"), sem("cqa_ps"), sem("cqb_ps")
        k_lat, k_step, k_hi = sem("k_lat"), sem("k_step"), sem("k_hi")
        v_ps, v_hi = sem("v_ps"), sem("v_hi")
        cq_hid, cq_lod = sem("cq_hid"), sem("cq_lod")
        q_ps, rope_mul, rope_sum, lat_out = sem("q_ps"), sem("rope_mul"), sem("rope_sum"), sem("lat_out")
        turned_out = [sem("turned_out_even"), sem("turned_out_odd")]
        q_split_hi, q_split_lo = sem("q_split_hi"), sem("q_split_lo")
        scores_ready, max_ready, exp_done = sem("scores_ready"), sem("max_ready"), sem("exp_done")
        pt_ps, pt_hi, pt_lo = sem("pt_ps"), sem("pt_hi"), sem("pt_lo")
        pv_done, rden_ready, row_ps, row_ready = sem("pv_done"), sem("rden_ready"), sem("row_ps"), sem("row_ready")
        wide_ready = sem("wide_ready")
        out_ready = sem("out_ready")
        fin_in = sem("fin_in")
        att_ps, att_res, ln_step, ln_pow = sem("att_ps"), sem("att_res"), sem("ln_step"), sem("ln_pow")
        x1_ready, x1T_ps, x1T_hid, x1T_lod = sem("x1_ready"), sem("x1T_ps"), sem("x1T_hid"), sem("x1T_lod")
        h_ps, silu_done, gate_done = sem("h_ps"), sem("silu_done"), sem("gate_done")
        ghi_done, glo_done, y_ps, y_res = sem("ghi_done"), sem("glo_done"), sem("y_ps"), sem("y_res")
        y_ready, y_out = sem("y_ready"), sem("y_out")

        block = ctx.enter_context(nc.Block())

        def hold(eng, s, value):
            eng.wait_ge(s, value)
            eng.sem_inc(held, 1)

        def end_phase(eng, k):
            eng.drain().then_inc(phase, 1)
            hold(eng, phase, 5 * k)

        @block.sync
        def _(sp):
            sp.dma_start(wuq_a[:, :], w_uq[0:P, :]).then_inc(w_qk_in, 16)
            sp.dma_start(wuq_b[:, :], w_uq[P:QR, :]).then_inc(w_qk_in, 16)
            sp.dma_start(wuk[:, :], w_uk).then_inc(w_qk_in, 16)
            sp.dma_start(wuv[:, :], w_uv).then_inc(w_qk_in, 16)
            sp.dma_start(wo[:, :, :], wo_v).then_inc(w_o_in, 16)
            sp.dma_start(wqr[:, 0, :], w_qr[0:P, :]).then_inc(w_qr_in, 16)
            sp.dma_start(wqr[0:64, 1, :], w_qr[P:QR, :]).then_inc(w_qr_in, 16)
            sp.dma_start(wqr[64:128, 1, :], w_qr[P:QR, :]).then_inc(w_qr_in, 16)
            sp.wait_ge(pad_ready, 3)
            for i, w in enumerate((w1, w3)):
                sp.dma_start(w13[:, i, 0:HT - 1, :],
                             w[0:(HT - 1) * P, :].rearrange("(t p) d -> p t d", p=P)).then_inc(w_ff_in, 16)
                sp.dma_start(w13[0:LAST, i, HT - 1, :], w[(HT - 1) * P:HID, :]).then_inc(w_ff_in, 16)
            sp.dma_start(w2n[:, :, 0:HID], w2.rearrange("(t p) h -> p t h", p=P)).then_inc(w_ff_in, 16)
            sp.wait_ge(ff_sb, 9)
            sp.dma_start(ternary, tern[:, :].bitcast(F)).then_inc(ff_out, 16)
            sp.wait_ge(ff_out, 16)
            end_phase(sp, 1)

            with sp.Fori(0, B) as b:
                sp.dma_start(xq[:, :, :], x_v[b]).then_inc(proj_in, 16)
                for kc in range(KC):
                    sp.dma_start(wkv_raw[:, kc, 0:DR], w_kr[kc * P:(kc + 1) * P, :]).then_inc(proj_in, 16)
                    sp.dma_start(wkv_raw[:, kc, DR:P], w_dkv[kc * P:(kc + 1) * P, :]).then_inc(proj_in, 16)
                    sp.dma_start(wdq[:, kc, :], w_dq[kc * P:(kc + 1) * P, :]).then_inc(proj_in, 16)
                sp.dma_start(tcos[:, :], cos).then_inc(proj_in, 16)
                sp.dma_start(tsin[:, :], sin).then_inc(proj_in, 16)
                for g in range(GROUPS):
                    sp.wait_ge(rope_sum, b * 2 * GROUPS + 2 * g + 2)
                    for s in range(4):
                        for j in range(2):
                            sp.dma_start(QO[32 * j:32 * j + 32, 4 * g + s, :],
                                         turned[32 * s:32 * s + 32, g % 2, j, :]).then_inc(turned_out[g % 2], 16)
                for parity in range(2):
                    hold(sp, turned_out[parity], b * 64 * GROUPS + 64 * GROUPS)
                end_phase(sp, 3 * b + 2)
                end_phase(sp, 3 * b + 3)
                sp.dma_start(xr[:, :, :], x_v[b]).then_inc(fin_in, 16)
                sp.dma_start(TT[:, :].bitcast(F), ternary).then_inc(fin_in, 16)
                for h in range(2):
                    sp.wait_ge(y_ready, b * 2 + h + 1)
                    sp.dma_start(out_v[b][:, 4 * h:4 * h + 4, :], yo[:, :, :]).then_inc(y_out, 16)
                hold(sp, y_out, b * 32 + 32)
                end_phase(sp, 3 * b + 4)

        @block.gpsimd
        def _(pool):
            nc.gpsimd.memset(ident[:, :], 0.0).then_inc(const_ready, 1)
            nc.gpsimd.memset(ones[:, :], 1.0).then_inc(const_ready, 1)
            nc.gpsimd.memset(minus_half[:, :], -0.5).then_inc(const_ready, 1)
            pool.wait_ge(const_ready, 3)
            nc.gpsimd.affine_select(out=ident[:, :], in_=ident[:, :], compare_op=ALU.not_equal, fill=1.0, base=0,
                                    pattern=[[-1, P]], channel_multiplier=1).then_inc(const_ready, 1)
            for i in range(2):
                nc.gpsimd.memset(w13[:, i, HT - 1, :], 0.0).then_inc(pad_ready, 1)
            nc.gpsimd.memset(w2n[:, :, HID:HT * P], 0.0).then_inc(pad_ready, 1)
            end_phase(pool, 1)

            with pool.Fori(0, B) as b:
                for g in range(GROUPS):
                    pool.wait_ge(rope_mul, b * 4 * GROUPS + 4 * g + 4)
                    if g >= 2:
                        pool.wait_ge(turned_out[g % 2], b * 64 * GROUPS + 64 * (g - g % 2))
                    nc.gpsimd.tensor_tensor(turned[:, g % 2, 0, :], qmul[:, 0, :], qmul[:, 1, :],
                                            ALU.subtract).then_inc(rope_sum, 1)
                    nc.gpsimd.tensor_tensor(turned[:, g % 2, 1, :], qmul[:, 2, :], qmul[:, 3, :],
                                            ALU.add).then_inc(rope_sum, 1)
                end_phase(pool, 3 * b + 2)

                def split_low(tile, pair, a):
                    pool.wait_ge(q_split_hi, pair * 2 + a + 1)
                    nc.gpsimd.tensor_tensor(Q_lo[:, a, :], QO[:, tile, :], Q_hi[:, a, :].bitcast(F),
                                            ALU.subtract).then_inc(q_split_lo, 1)

                def widen(group, h):
                    hold(pool, rden_ready, group + 1)
                    src = rden[:, h].rearrange("p a t -> p t a").unsqueeze(3).broadcast_to([P, 4, 2, KVR])
                    nc.gpsimd.tensor_scalar(rden_wide[:, :, :, :], src, 1.0, 1.0, ALU.mult,
                                            ALU.mult).then_inc(wide_ready, 1)

                def pair_pool(p, first, last):
                    pair = b * PAIRS + p
                    if not first:
                        widen(pair * 2 - 1, 1)
                    widen(pair * 2, 0)
                    if not last:
                        for a in range(2):
                            split_low(p * 2 + 2 + a, pair + 1, a)

                for a in range(2):
                    split_low(a, b * PAIRS, a)
                pair_pool(0, True, False)
                with pool.Fori(1, PAIRS - 1) as p:
                    pair_pool(p, False, False)
                pair_pool(PAIRS - 1, False, True)
                widen(b * PAIRS * 2 + 2 * PAIRS - 1, 1)
                end_phase(pool, 3 * b + 3)

                def power(h, n):
                    pool.wait_ge(ln_step, n)
                    nc.gpsimd.tensor_tensor(rstd[:, 4 * h:4 * h + 4], ve[:, 4 * h:4 * h + 4], minus_half[:, :],
                                            ALU.pow).then_inc(ln_pow, 1)

                for h in range(2):
                    power(h, b * 4 + h + 1)
                for h in range(2):
                    for t in range(HT):
                        pool.wait_ge(ghi_done, b * 2 * HT + HT * h + t + 1)
                        nc.gpsimd.tensor_tensor(g_lo[:, t, :], gate[:, t % 2, :], g_hi[:, t, :].bitcast(F),
                                                ALU.subtract).then_inc(glo_done, 1)
                    power(h, b * 4 + 3 + h)
                end_phase(pool, 3 * b + 4)

        @block.scalar
        def _(act_):
            def copy(o, i, scale=1.0):
                return nc.scalar.activation(o, i, ACT.Copy, scale=scale)

            act_.sem_inc(exp_done, EXP0)
            act_.sem_inc(row_ready, ROW0)

            def weights_out(h):
                act_.wait_ge(wt_ps, h + 1)
                if h >= 2:
                    act_.wait_ge(prod_ps, h - 1)
                copy(wT[:, h % 2, :], TS[h % 2][:, 0:384]).then_inc(wt_sb, 1)

            def product_high(j):
                act_.wait_ge(prod_ps, 2 * j + 2)
                tile = 4 * (j // 2) + 2 + j % 2
                copy(Wq_hi[:, tile, :, :], OS[j % 2][:, 0:256].rearrange("p (c m) -> p c m", c=2)).then_inc(prod_hi, 1)

            weights_out(0)
            weights_out(1)
            for h in range(2, H):
                weights_out(h)
                if h % 2 == 0:
                    product_high(h // 2 - 1)
            product_high(PAIRS - 1)
            act_.wait_ge(w_qr_in, 48)
            for j in range(2):
                for c in range(2):
                    src = wqr[:, c, :].rearrange("p (g m two) -> p two g m", two=2, m=P)[:, j]
                    copy(Wq_hi[:, j::4, c, :], src).then_inc(qr_hi, 1)
            for n in range(9):
                act_.wait_ge(ff_ps, n + 1)
                copy(tern[:, n * 512:(n + 1) * 512], (Sa, Sb)[n // 2 % 2][:, n % 2 * 512:n % 2 * 512 + 512]).then_inc(ff_sb, 1)
            end_phase(act_, 1)

            with act_.Fori(0, B) as b:
                for n in range(4):
                    act_.wait_ge(xT_ps, b * 4 + n + 1)
                    copy(xT[:, n % 2, n // 2 * HALF:(n // 2 + 1) * HALF], (Ta, Tb, Oa, Ob)[n][:, :]).then_inc(xT_sb, 1)
                act_.wait_ge(kv_ps, b + 1)
                copy(Kf[64:128, :], Sa[64:128, :]).then_inc(k_lat, 1)
                act_.wait_ge(cqa_ps, b + 1)
                copy(cq_hi[:, :], Sb[:, :], SCALE).then_inc(cq_hid, 1)
                act_.wait_ge(cqb_ps, b + 1)
                for n in range(2):
                    copy(cq_s[:, n * HALF:(n + 1) * HALF], TS[n][:, :], SCALE).then_inc(cq_hid, 1)
                act_.wait_ge(k_lat, b + 1)
                act_.wait_ge(k_step, b * 11 + 4)
                copy(K_hi[:, :], Kf[:, :]).then_inc(k_hi, 1)
                act_.wait_ge(v_ps, b + 1)
                copy(V_hi[:, :, :], Oa[:, :].rearrange("p (k c) -> p k c", k=KT)).then_inc(v_hi, 1)
                for g in range(GROUPS):
                    for i in range(2):
                        act_.wait_ge(q_ps, b * 4 * GROUPS + 4 * g + 3 + i)
                        for n in range(2):
                            for a in range(2):
                                bank = (TS, OS)[i][n]
                                copy(QO[64:128, 4 * g + 2 * i + a, n * HALF:(n + 1) * HALF],
                                     bank[64 * a:64 * a + 64, :]).then_inc(lat_out, 1)
                end_phase(act_, 3 * b + 2)

                def split_high(tile, pair, a, free):
                    if free is not None:
                        act_.wait_ge(scores_ready, free)
                    copy(Q_hi[:, a, :], QO[:, tile, :]).then_inc(q_split_hi, 1)

                def exponent(tile, n):
                    act_.wait_ge(max_ready, tile + 1)
                    act_.wait_ge(pt_ps, tile * 2 + 2)
                    nc.scalar.activation(probs[:, n % 2, :], SS[n % 2][:, :], ACT.Exp, bias=nmax[:, n % 4:n % 4 + 1],
                                         accum_out=den[:, n // 8 % 2, n // 4 % 2, n % 4:n % 4 + 1]).then_inc(exp_done, 1)

                def transposed_high(tile, n):
                    for j in range(2):
                        act_.wait_ge(pt_ps, PT0 + tile * 2 + j + 1)
                        dst = PT_hi[:, n // 8, n // 4 % 2, 4 * j:4 * j + 4, n % 4 * P:n % 4 * P + P]
                        copy(dst, TS[j][:, :].rearrange("p (k q) -> p k q", k=4), PROB_UP).then_inc(pt_hi, 1)

                def row_out(group):
                    act_.wait_ge(row_ps, group + 1)
                    act_.wait_ge(out_ready, group + 1)
                    copy(rden_row[:, :], Ob[:, :]).then_inc(row_ready, 1)

                def pair_act(p, first, last):
                    pair = b * PAIRS + p
                    t0 = pair * TILES
                    for n in range(TILES):
                        if not (last and n == TILES - 1):
                            exponent(t0 + n + 1, n + 1)
                        transposed_high(t0 + n, n)
                        if n in (3, 11) and not (first and n == 3):
                            row_out(pair * 2 + (n // 8) - 1)
                        if n in (10, 14) and not last:
                            split_high(p * 2 + 2 + n // 12, pair + 1, n // 12, t0 + (12 if n == 10 else 16))

                for a in range(2):
                    split_high(a, b * PAIRS, a, None)
                exponent(b * PAIRS * TILES, 0)
                pair_act(0, True, False)
                with act_.Fori(1, PAIRS - 1) as p:
                    pair_act(p, False, False)
                pair_act(PAIRS - 1, False, True)
                row_out(b * PAIRS * 2 + 2 * PAIRS - 1)
                end_phase(act_, 3 * b + 3)

                def x1_high(h):
                    act_.wait_ge(x1T_ps, b * 2 + h + 1)
                    copy(x1T_hi[:, :, :], Sa[:, :].rearrange("p (c q) -> p c q", c=2)).then_inc(x1T_hid, 1)

                for h in range(2):
                    x1_high(h)
                    for t in range(HT):
                        u = b * 2 * HT + HT * h + t
                        act_.wait_ge(h_ps, u + 1)
                        if HT * h + t >= 2:
                            act_.wait_ge(gate_done, u - 1)
                        bank = (Ta, Oa)[t % 2]
                        nc.scalar.activation(act[:, t % 2, :], bank[:, :], ACT.Silu, scale=ffs[:, 0:1]).then_inc(silu_done, 1)
                        act_.wait_ge(gate_done, u + 1)
                        if h == 1 and t == 0:
                            act_.wait_ge(y_ps, b * 8 + 4)
                        copy(g_hi[:, t, :], gate[:, t % 2, :]).then_inc(ghi_done, 1)
                end_phase(act_, 3 * b + 4)

        @block.vector
        def _(dve):
            dve.sem_inc(pt_lo, LO0)
            dve.sem_inc(out_ready, OUT0)

            for j in range(PAIRS):
                dve.wait_ge(prod_hi, j + 1)
                tile = 4 * (j // 2) + 2 + j % 2
                bank = OS[j % 2]
                nc.vector.tensor_tensor(Wq_lo[:, tile, :, :], bank[:, 0:256].rearrange("p (c m) -> p c m", c=2),
                                        Wq_hi[:, tile, :, :].bitcast(F), ALU.subtract)
                nc.vector.tensor_copy(Wvo[:, j, :], bank[:, 256:512]).then_inc(prod_lo, 1)
            for j in range(2):
                for c in range(2):
                    dve.wait_ge(qr_hi, 2 * j + c + 1)
                    src = wqr[:, c, :].rearrange("p (g m two) -> p two g m", two=2, m=P)[:, j]
                    nc.vector.tensor_tensor(Wq_lo[:, j::4, c, :], src, Wq_hi[:, j::4, c, :].bitcast(F), ALU.subtract)
            dve.wait_ge(w_ff_in, 80)
            dve.wait_ge(pad_ready, 3)
            for i in range(3):
                src = w13[:, i, :, :] if i < 2 else w2n[:, :, :]
                nc.vector.tensor_reduce(asum[:, i:i + 1], src, AX.XY, ALU.add, apply_absolute_value=True).then_inc(ff_sum, 1)
            dve.wait_ge(ff_mean, 1)
            nc.vector.tensor_scalar(ffs[:, 0:3], Ob[:, 0:3], 1.0 / (HID * D), None, ALU.mult).then_inc(ff_step, 1)
            dve.wait_ge(ff_step, 1)
            nc.vector.tensor_scalar(ffs[:, 3:6], ffs[:, 0:3], 0.5, None, ALU.mult).then_inc(ff_step, 1)
            nc.vector.tensor_tensor(ffs[:, 6:7], ffs[:, 1:2], ffs[:, 2:3], ALU.mult).then_inc(ff_step, 1)
            dve.wait_ge(ff_step, 3)
            for i in range(3):
                w = (w13[:, i, :, :].rearrange("p t d -> p (t d)") if i < 2
                     else w2n[:, :, :].rearrange("p t h -> p (t h)"))
                if i:
                    dve.wait_ge(ff_tern, i)
                nc.vector.tensor_scalar(below[:, :], w, -1.0, ffs[:, 3 + i:4 + i], ALU.mult, ALU.is_gt).then_inc(ff_step, 1)
                dve.wait_ge(ff_step, 4 + i)
                nc.vector.scalar_tensor_tensor(w, w, ffs[:, 3 + i:4 + i], below[:, :], ALU.is_gt,
                                               ALU.subtract).then_inc(ff_tern, 1)
            end_phase(dve, 1)

            with dve.Fori(0, B) as b:
                dve.wait_ge(proj_in, b * 144 + 144)
                nc.vector.tensor_copy(wkv[:, :, 0:DR].rearrange("p c (two i) -> p c two i", two=2),
                                      wkv_raw[:, :, 0:DR].rearrange("p c (i two) -> p c two i", two=2)).then_inc(w_small, 1)
                nc.vector.tensor_copy(wkv[:, :, DR:P], wkv_raw[:, :, DR:P]).then_inc(w_small, 1)
                for a in range(2):
                    nc.vector.tensor_copy(wdq_b[:, :, a, :], wdq[:, :, P:QR]).then_inc(w_small, 1)

                K0 = b * 11
                dve.wait_ge(kv_ps, b + 1)
                nc.vector.tensor_tensor(kmul[0:64, 0, :], Sa[0:64, :], tcos[0:64, :], ALU.mult)
                nc.vector.tensor_tensor(kmul[32:64, 1, :], Sa[0:32, :], tsin[0:32, :], ALU.mult).then_inc(k_step, 1)
                nc.vector.tensor_tensor(kmul[0:32, 1, :], Sa[32:64, :], tsin[32:64, :], ALU.mult).then_inc(k_step, 1)
                dve.wait_ge(k_step, K0 + 2)
                nc.vector.tensor_tensor(Kf[0:32, :], kmul[0:32, 0, :], kmul[0:32, 1, :], ALU.subtract).then_inc(k_step, 1)
                nc.vector.tensor_tensor(Kf[32:64, :], kmul[32:64, 0, :], kmul[32:64, 1, :], ALU.add).then_inc(k_step, 1)
                dve.wait_ge(k_lat, b + 1)
                nc.vector.tensor_reduce(vscale[64:128, 0:1], Kf[64:128, :], AX.X, ALU.max,
                                        apply_absolute_value=True).then_inc(k_step, 1)
                dve.wait_ge(k_step, K0 + 5)
                nc.vector.tensor_scalar(vscale[64:128, 1:2], vscale[64:128, 0:1], 1e-30, None, ALU.max).then_inc(k_step, 1)
                dve.wait_ge(k_step, K0 + 6)
                nc.vector.tensor_scalar(vscale[64:128, 0:1].bitcast(I32), vscale[64:128, 1:2].bitcast(I32),
                                        0x7F800000, None, ALU.bitwise_and).then_inc(k_step, 1)
                dve.wait_ge(k_step, K0 + 7)
                nc.vector.reciprocal(vscale[64:128, 2:3], vscale[64:128, 0:1]).then_inc(k_step, 1)
                nc.vector.tensor_scalar(vscale[64:128, 3:4], vscale[64:128, 0:1], 1.0 / (PROB_UP * VAL_UP), None,
                                        ALU.mult).then_inc(k_step, 1)
                dve.wait_ge(k_step, K0 + 9)
                nc.vector.tensor_copy(vscale[0:64, 3:4], vscale[64:128, 3:4])
                nc.vector.tensor_scalar(kmul[64:128, 0, :], Kf[64:128, :], vscale[64:128, 2:3], VAL_UP, ALU.mult,
                                        ALU.mult).then_inc(k_step, 1)
                dve.wait_ge(cq_hid, b * 3 + 1)
                nc.vector.scalar_tensor_tensor(cq_lo[:, :], Sb[:, :], SCALE, cq_hi[:, :].bitcast(F), ALU.mult,
                                               ALU.subtract).then_inc(cq_lod, 1)
                dve.wait_ge(cq_hid, b * 3 + 3)
                for n in range(2):
                    low = cq_s[64:128, n * HALF:(n + 1) * HALF]
                    nc.vector.scalar_tensor_tensor(low, TS[n][64:128, :], SCALE, low.bitcast(F), ALU.mult,
                                                   ALU.subtract).then_inc(cq_lod, 1)
                dve.wait_ge(k_hi, b + 1)
                nc.vector.tensor_tensor(K_lo[:, :], Kf[:, :], K_hi[:, :].bitcast(F), ALU.subtract).then_inc(k_step, 1)
                dve.wait_ge(v_hi, b + 1)
                nc.vector.tensor_tensor(V_lo[:, :, :], Oa[:, :].rearrange("p (k c) -> p k c", k=KT), V_hi[:, :, :],
                                        ALU.subtract).then_inc(cq_lod, 1)
                for g in range(GROUPS):
                    for j, (tile, table, dst) in enumerate(((0, tcos, 0), (0, tsin, 2), (1, tsin, 1), (1, tcos, 3))):
                        if tile == j // 2 and j % 2 == 0:
                            dve.wait_ge(q_ps, b * 4 * GROUPS + 4 * g + tile + 1)
                        if g >= 1:
                            dve.wait_ge(rope_sum, b * 2 * GROUPS + 2 * g)
                        nc.vector.tensor_tensor(qmul[:, dst, :], SS[tile][:, :], table[:, :], ALU.mult).then_inc(rope_mul, 1)
                end_phase(dve, 3 * b + 2)

                def maximum(tile, n):
                    dve.wait_ge(scores_ready, tile + 1)
                    nc.vector.tensor_reduce(nmax[:, n % 4:n % 4 + 1], SS[n % 2][:, :], AX.X, ALU.max,
                                            negate=True).then_inc(max_ready, 1)

                def transposed_low(tile, n):
                    for j in range(2):
                        dve.wait_ge(pt_hi, tile * 2 + j + 1)
                        place = (slice(None), n // 8, n // 4 % 2, slice(4 * j, 4 * j + 4), slice(n % 4 * P, n % 4 * P + P))
                        nc.vector.scalar_tensor_tensor(PT_lo[place], TS[j][:, :].rearrange("p (k q) -> p k q", k=4),
                                                       PROB_UP, PT_hi[place], ALU.mult, ALU.subtract).then_inc(pt_lo, 1)

                def reciprocal(group, h):
                    dve.wait_ge(exp_done, EXP0 + group * 8 + 8)
                    nc.vector.reciprocal(rden[:, h], den[:, h]).then_inc(rden_ready, 1)

                def normalise(group, pair_row, h):
                    dve.wait_ge(pv_done, group + 1)
                    dve.wait_ge(row_ready, ROW0 + group + 1)
                    nc.vector.scalar_tensor_tensor(QO[:, pair_row, h * HALF:(h + 1) * HALF], Oa[:, :], vscale[:, 3:4],
                                                   rden_row[:, :], ALU.mult, ALU.mult).then_inc(out_ready, 1)

                def pair_dve(p, first, last):
                    pair = b * PAIRS + p
                    t0 = pair * TILES
                    for n in range(TILES):
                        h = n // 8
                        if n % 8 == 0:
                            if not first:
                                normalise(pair * 2 + h - 2, p * 2 - 2, h)
                            if not (first and h == 0):
                                reciprocal(pair * 2 + h - 1, 1 - h)
                        if not (last and n >= TILES - 2):
                            maximum(t0 + n + 2, n + 2)
                        transposed_low(t0 + n, n)

                for n in range(2):
                    maximum(b * PAIRS * TILES + n, n)
                pair_dve(0, True, False)
                with dve.Fori(1, PAIRS - 1) as p:
                    pair_dve(p, False, False)
                pair_dve(PAIRS - 1, False, True)
                group = b * PAIRS * 2 + 2 * PAIRS
                normalise(group - 2, 2 * PAIRS - 2, 0)
                reciprocal(group - 1, 1)
                normalise(group - 1, 2 * PAIRS - 2, 1)
                end_phase(dve, 3 * b + 3)

                def statistics(t, n):
                    nc.vector.bn_stats(stats[:, t, :], res[:, t, :]).then_inc(att_res, 1)
                    hold(dve, att_res, n + 2)
                    nc.vector.bn_aggr(mv[:, t, :], stats[:, t, :]).then_inc(att_res, 1)

                def add_eps(h, n):
                    dve.wait_ge(att_res, n)
                    nc.vector.tensor_scalar(ve[:, 4 * h:4 * h + 4], mv[:, 4 * h:4 * h + 4, 1], EPS, None,
                                            ALU.add).then_inc(ln_step, 1)

                dve.wait_ge(fin_in, b * 32 + 32)
                A0 = b * 48
                for t in range(QT):
                    dve.wait_ge(att_ps, b * 8 + t + 1)
                    nc.vector.tensor_tensor(res[:, t, :], (Ta, Tb, Oa, Ob)[t % 4][:, 0:D], xr[:, t, :],
                                            ALU.add).then_inc(att_res, 1)
                    dve.wait_ge(att_res, A0 + 3 * t + 1)
                    statistics(t, A0 + 3 * t)
                    if t % 4 == 3:
                        add_eps(t // 4, A0 + 3 * t + 3)
                for h in range(2):
                    dve.wait_ge(ln_pow, b * 4 + h + 1)
                    for t in range(4 * h, 4 * h + 4):
                        nc.vector.tensor_scalar(x1[:, t, :], res[:, t, :], mv[:, t, 0:1], rstd[:, t:t + 1],
                                                ALU.subtract, ALU.mult).then_inc(x1_ready, 1)
                for h in range(2):
                    dve.wait_ge(x1T_hid, b * 2 + h + 1)
                    nc.vector.tensor_tensor(x1T_lo[:, :, :], Sa[:, :].rearrange("p (c q) -> p c q", c=2),
                                            x1T_hi[:, :, :].bitcast(F), ALU.subtract).then_inc(x1T_lod, 1)
                    for t in range(HT):
                        u = b * 2 * HT + HT * h + t
                        dve.wait_ge(silu_done, u + 1)
                        if HT * h + t >= 2:
                            dve.wait_ge(glo_done, u - 1)
                        bank = (Tb, Ob)[t % 2]
                        nc.vector.tensor_tensor(gate[:, t % 2, :], bank[:, :], act[:, t % 2, :], ALU.mult).then_inc(gate_done, 1)
                    for t in range(4 * h, 4 * h + 4):
                        n = A0 + 24 + 3 * t
                        dve.wait_ge(y_ps, b * 8 + t + 1)
                        nc.vector.scalar_tensor_tensor(res[:, t, :], Sb[:, t % 2 * HALF:t % 2 * HALF + D], ffs[:, 6:7],
                                                       x1[:, t, :], ALU.mult, ALU.add).then_inc(att_res, 1)
                        dve.wait_ge(att_res, n + 1)
                        statistics(t, n)
                    add_eps(h, A0 + 24 + 12 * h + 12)
                    dve.wait_ge(ln_pow, b * 4 + 3 + h)
                    if h == 1:
                        dve.wait_ge(y_out, b * 32 + 16)
                    for t in range(4):
                        last = nc.vector.tensor_scalar(yo[:, t, :], res[:, 4 * h + t, :], mv[:, 4 * h + t, 0:1],
                                                       rstd[:, 4 * h + t:4 * h + t + 1], ALU.subtract, ALU.mult)
                    last.then_inc(y_ready, 1)
                end_phase(dve, 3 * b + 4)

        @block.tensor
        def _(pe):
            mm = nc.tensor.matmul
            pe.sem_inc(pt_ps, PT0)

            pe.wait_ge(const_ready, 4)
            pe.wait_ge(w_qk_in, 64)

            def turn_weights(h):
                if h >= 2:
                    pe.wait_ge(wt_sb, h - 1)
                bank, cols = TS[h % 2], slice(h * DN, (h + 1) * DN)
                nc.tensor.transpose(bank[:, 0:128], wuq_a[:, cols], ident[:, :])
                nc.tensor.transpose(bank[:, 128:192], wuq_b[:, cols], ident[0:64, 0:64])
                nc.tensor.transpose(bank[:, 192:256], wuq_b[:, cols], ident[0:64, 0:64])
                nc.tensor.transpose(bank[:, 256:320], wuk[:, cols], ident[0:64, 0:64])
                nc.tensor.transpose(bank[:, 320:384], wuv[:, cols], ident[0:64, 0:64]).then_inc(wt_ps, 1)

            def weight_products(h):
                pe.wait_ge(wt_sb, h + 1)
                j, a = h // 2, h % 2
                if a == 0 and j >= 2:
                    pe.wait_ge(prod_lo, j - 1)
                w, bank = wT[:, a, :], OS[j % 2]
                mm(bank[:, 64 * a:64 * a + 64], w[:, 0:128], w[:, 256:320], start=True, stop=True)
                mm(bank[:, 128 + 64 * a:192 + 64 * a], w[:, 128:256], w[:, 256:320], start=True, stop=True)
                mm(bank[64 * a:64 * a + 64, 256:512], w[:, 320:384], wo[:, h, :], start=True, stop=True).then_inc(prod_ps, 1)

            turn_weights(0)
            turn_weights(1)
            pe.wait_ge(w_o_in, 16)
            for h in range(H):
                weight_products(h)
                if h + 2 < H:
                    turn_weights(h + 2)
            pe.wait_ge(ff_sum, 3)
            pe.wait_ge(prod_lo, PAIRS)
            mm(Ob[:, 0:3], ones[:, :], asum[:, 0:3], start=True, stop=True).then_inc(ff_mean, 1)
            for n in range(9):
                pe.wait_ge(ff_tern, n // 3 + 1)
                if n >= 4:
                    pe.wait_ge(ff_sb, n - 3)
                bank = (Sa, Sb)[n // 2 % 2]
                for k in range(4):
                    i = 4 * (n % 3) + k
                    if n < 6:
                        src = w13[:, n // 3, i % HT, i // HT * P:i // HT * P + P]
                    else:
                        src = w2n[:, i % KC, i // KC * P:i // KC * P + P]
                    last = nc.tensor.transpose(bank[:, n % 2 * 512 + k * P:n % 2 * 512 + k * P + P], src, ident[:, :])
                last.then_inc(ff_ps, 1)
            end_phase(pe, 1)

            with pe.Fori(0, B) as b:
                pe.wait_ge(proj_in, b * 144 + 144)
                for n in range(4):
                    for t in range(4):
                        last = nc.tensor.transpose((Ta, Tb, Oa, Ob)[n][:, t * P:(t + 1) * P],
                                                   xq[:, n // 2 * 4 + t, n % 2 * P:n % 2 * P + P], ident[:, :])
                    last.then_inc(xT_ps, 1)
                pe.wait_ge(w_small, b * 4 + 4)
                pe.wait_ge(xT_sb, b * 4 + 4)

                def project(outs, lhs, signal):
                    for kc in range(KC):
                        for n in range(2):
                            last = mm(outs[n], lhs(kc), xT[:, kc, n * HALF:(n + 1) * HALF],
                                      start=(kc == 0), stop=(kc == KC - 1))
                    last.then_inc(signal, 1)

                project((Sa[:, 0:HALF], Sa[:, HALF:S]), lambda kc: wkv[:, kc, :], kv_ps)
                project((Sb[:, 0:HALF], Sb[:, HALF:S]), lambda kc: wdq[:, kc, 0:P], cqa_ps)
                project((Ta[:, :], Tb[:, :]), lambda kc: wdq_b[:, kc, :, :], cqb_ps)
                hold(pe, k_step, b * 11 + 10)
                for k in range(KT):
                    last = nc.tensor.transpose(Oa[:, k * KVR:(k + 1) * KVR], kmul[64:128, 0, k * P:(k + 1) * P],
                                               ident[64:128, 64:128])
                last.then_inc(v_ps, 1)
                pe.wait_ge(cq_lod, b * 4 + 3)
                for g in range(GROUPS):
                    for j in range(4):
                        if g == 0 and j == 3:
                            pe.wait_ge(cq_lod, b * 4 + 4)
                        if g >= 1 and j < 2:
                            pe.wait_ge(rope_mul, b * 4 * GROUPS + 4 * g - 2 + 2 * j)
                        if g >= 1 and j >= 2:
                            pe.wait_ge(lat_out, b * 8 * GROUPS + 8 * g - 4 + 4 * (j - 2))
                        outs = ((Sa[:, 0:HALF], Sa[:, HALF:S]), (Sb[:, 0:HALF], Sb[:, HALF:S]),
                                (Ta[:, :], Tb[:, :]), (Oa[:, :], Ob[:, :]))[j]
                        t = 4 * g + j
                        terms = ((Wq_hi[:, t, 0, :], cq_hi), (Wq_hi[:, t, 0, :], cq_lo), (Wq_lo[:, t, 0, :], cq_hi),
                                 (Wq_hi[:, t, 1, :], cq_s), (Wq_lo[:, t, 1, :], cq_s))
                        for k, (w, c) in enumerate(terms):
                            for n in range(2):
                                last = mm(outs[n], w, c[:, n * HALF:(n + 1) * HALF], start=(k == 0), stop=(k == 4))
                        last.then_inc(q_ps, 1)
                end_phase(pe, 3 * b + 2)

                def scores(tile, n, pair):
                    a, q = n // 4 % 2, (n // 8 * 4 + n % 4) * P
                    if n in (0, 4):
                        pe.wait_ge(q_split_lo, pair * 2 + a + 1)
                    pe.wait_ge(exp_done, tile + 1)
                    bank = SS[n % 2]
                    for k, (w, c) in enumerate(((Q_hi, K_hi), (Q_hi, K_lo), (Q_lo, K_hi))):
                        for m in range(2):
                            last = mm(bank[:, m * HALF:(m + 1) * HALF], w[:, a, q:q + P], c[:, m * HALF:(m + 1) * HALF],
                                      start=(k == 0), stop=(k == 2))
                    last.then_inc(scores_ready, 1)

                def transpose_probs(tile, n):
                    pe.wait_ge(exp_done, EXP0 + tile + 1)
                    for j in range(2):
                        pe.wait_ge(pt_lo, tile * 2 + j + 1)
                        for k in range(4):
                            last = nc.tensor.transpose(TS[j][:, k * P:(k + 1) * P],
                                                       probs[:, n % 2, (4 * j + k) * P:(4 * j + k + 1) * P], ident[:, :])
                        last.then_inc(pt_ps, 1)

                def values(group, h, k):
                    if k == 0:
                        pe.wait_ge(pt_lo, LO0 + group * 16 + 16)
                        pe.wait_ge(out_ready, group + 1)
                    for i, (v, pt) in enumerate(((V_hi, PT_hi), (V_lo, PT_hi), (V_hi, PT_lo))):
                        for a in range(2):
                            last = mm(Oa[64 * a:64 * a + 64, :], v[:, k, :], pt[:, h, a, k, :],
                                      start=(k == 0 and i == 0), stop=(k == KT - 1 and i == 2))
                    if k == KT - 1:
                        last.then_inc(pv_done, 1)

                def sums_to_rows(group):
                    pe.wait_ge(wide_ready, group + 1)
                    pe.wait_ge(row_ready, group + 1)
                    for t in range(4):
                        last = nc.tensor.transpose(Ob[:, t * P:(t + 1) * P], rden_wide[:, t], ident[:, :])
                    last.then_inc(row_ps, 1)

                def pair_pe(p, first, last):
                    pair = b * PAIRS + p
                    t0 = pair * TILES
                    for n in range(TILES):
                        if not (last and n >= TILES - 2):
                            scores(t0 + n + 2, (n + 2) % TILES, pair + (n + 2) // TILES)
                        transpose_probs(t0 + n, n)
                        if not (first and n < 8):
                            values(pair * 2 + n // 8 - 1, 1 - n // 8, n % 8)
                            if n % 8 == 2:
                                sums_to_rows(pair * 2 + n // 8 - 1)

                for n in range(2):
                    scores(b * PAIRS * TILES + n, n, b * PAIRS)
                pair_pe(0, True, False)
                with pe.Fori(1, PAIRS - 1) as p:
                    pair_pe(p, False, False)
                pair_pe(PAIRS - 1, False, True)
                group = b * PAIRS * 2 + 2 * PAIRS - 1
                sums_to_rows(group)
                for k in range(KT):
                    values(group, 1, k)
                end_phase(pe, 3 * b + 3)

                for t in range(QT):
                    if t >= 4:
                        pe.wait_ge(att_res, b * 48 + 3 * (t - 4) + 1)
                    for j in range(PAIRS):
                        last = mm((Ta, Tb, Oa, Ob)[t % 4][:, 0:D], QO[:, 2 * j, t * P:(t + 1) * P], Wvo[:, j, :],
                                  start=(j == 0), stop=(j == PAIRS - 1))
                    last.then_inc(att_ps, 1)

                def turn_x1(h):
                    pe.wait_ge(x1_ready, b * 8 + 4 * h + 4)
                    if h:
                        pe.wait_ge(x1T_lod, b * 2 + 1)
                    for t in range(4):
                        for c in range(KC):
                            last = nc.tensor.transpose(Sa[:, c * HALF + t * P:c * HALF + (t + 1) * P],
                                                       x1[:, 4 * h + t, c * P:(c + 1) * P], ident[:, :])
                    last.then_inc(x1T_ps, 1)

                def hidden(h, t):
                    u = b * 2 * HT + HT * h + t
                    if HT * h + t >= 2:
                        pe.wait_ge(gate_done, u - 1)
                    elif t == 0:
                        pe.wait_ge(att_res, b * 48 + 24)
                    for i in range(2):
                        bank = ((Ta, Tb), (Oa, Ob))[t % 2][i]
                        for k in range(4):
                            w = TT[:, (i * 2 * HT + k // 2 * HT + t) * P:(i * 2 * HT + k // 2 * HT + t + 1) * P]
                            last = mm(bank[:, :], w, (x1T_hi, x1T_lo)[k % 2][:, k // 2, :], start=(k == 0), stop=(k == 3))
                    last.then_inc(h_ps, 1)

                def down(t, h):
                    if t >= 2:
                        pe.wait_ge(att_res, b * 48 + 24 + 3 * (t - 2) + 1)
                    for i in range(HT):
                        w = TT[:, 4 * HT * P + i * D:4 * HT * P + (i + 1) * D]
                        for k in range(2):
                            last = mm(Sb[:, t % 2 * HALF:t % 2 * HALF + D], (g_hi, g_lo)[k][:, i, t % 4 * P:t % 4 * P + P], w,
                                      start=(i == 0 and k == 0), stop=(i == HT - 1 and k == 1))
                    last.then_inc(y_ps, 1)

                pe.wait_ge(fin_in, b * 32 + 32)
                for h in range(2):
                    turn_x1(h)
                    pe.wait_ge(x1T_lod, b * 2 + h + 1)
                    for t in range(HT):
                        hidden(h, t)
                    pe.wait_ge(glo_done, b * 2 * HT + HT * h + HT)
                    for t in range(4 * h, 4 * h + 4):
                        down(t, h)
                end_phase(pe, 3 * b + 4)


_INS = ['L0_attn_x', 'L0_attn_w_dkv', 'L0_attn_w_kr', 'L0_attn_w_uk', 'L0_attn_w_uv', 'L0_attn_w_dq',
        'L0_attn_w_qr', 'L0_attn_w_uq', 'L0_attn_w_o', 'L0_ffn_w1', 'L0_ffn_w3', 'L0_ffn_w2']


def kernel(**inputs):
    import concourse.bacc as _bacc
    from concourse.bass_utils import run_bass_kernel_spmd as _run

    nc = _bacc.Bacc("TRN2", target_bir_lowering=False, num_devices=1)
    arrays, args = {}, []
    cos, sin = rope_tables()
    given = [(f"in_{n}_dram", inputs[n]) for n in _INS] + [("rope_cos", cos), ("rope_sin", sin)]
    for name, a in given:
        a = np.ascontiguousarray(a)
        arrays[name] = a
        args.append(nc.dram_tensor(name, a.shape, mybir.dt.from_np(a.dtype), kind="ExternalInput").ap())
    args.append(nc.dram_tensor("out_dram", (B, S, D), mybir.dt.float32, kind="ExternalOutput").ap())
    build(nc, *args)
    r = _run(nc, [arrays], core_ids=[0])
    return r.results[0]["out_dram"]
```

```python
import math
from contextlib import ExitStack

import numpy as np

import concourse.bass as bass
from concourse import mybir

B, S, D = 2, 1024, 256
H, DR, DN, DV = 16, 64, 128, 128
KVR, QR = 64, 192
HID = 682
THETA = 10000.0
EPS = 1e-5
P = 128
QT = S // P
KT = S // P
KC = D // P
PAIRS = H // 2
HALF = S // 2
GROUPS = 4
HT = -(-HID // P)
LAST = HID - (HT - 1) * P
W = 3 * HT * D
PROB_UP = 2.0 ** 14
VAL_UP = 2.0 ** 8
TILES = 4 * 4

EXP0, PT0, LO0, PV0, OUT0, ROW0, Y0, STORED0 = 2, 4, 2, 1, 1, 1, 2, 1


def rope_tables():
    inv = np.float32(1.0) / np.float32(THETA) ** (np.arange(0, DR, 2, dtype=np.float32) / np.float32(DR))
    ang = np.arange(S, dtype=np.float32)[:, None] * inv[None, :].astype(np.float32)
    cos = np.cos(ang.astype(np.float64)).astype(np.float32).T
    sin = np.sin(ang.astype(np.float64)).astype(np.float32).T
    return np.ascontiguousarray(np.tile(cos, (4, 1))), np.ascontiguousarray(np.tile(sin, (4, 1)))


def build(nc, x, w_dkv, w_kr, w_uk, w_uv, w_dq, w_qr, w_uq, w_o, w1, w3, w2, cos, sin, out):
    F = mybir.dt.float32
    R = mybir.dt.float32r
    F16 = mybir.dt.float16
    I32 = mybir.dt.int32
    ALU = mybir.AluOpType
    ACT = mybir.ActivationFunctionType
    AX = mybir.AxisListType
    SCALE = 1.0 / math.sqrt(DR + DN)

    x_v = x.rearrange("b (t p) d -> b p t d", p=P)
    out_v = out.rearrange("b (t p) d -> b p t d", p=P)
    wo_v = w_o.rearrange("(h n) d -> n h d", n=DV)
    ternary = nc.dram_tensor("ternary", [P, W], F, kind="Internal").ap()

    ctx = ExitStack()
    with ctx:
        def sem(name):
            return ctx.enter_context(nc.semaphore(name))

        def sb(stack, name, shape, dt):
            return stack.enter_context(nc.sbuf_tensor(name, shape, dt))

        base = -(-nc.sbuf_base // 64) * 64
        arena = sb(ctx, "arena", [P, (nc.sbuf_usable_end - base) // 4 - 32], F)
        top = [0]

        def lay(start, *tensors):
            made, at = [], start
            for name, shape, dt in tensors:
                made.append(nc.alloc_sbuf_tensor_at(name, shape, dt, offset=base + at))
                at += -(-math.prod(shape[1:]) * (2 if dt == F16 else 4) // 64) * 64
            top[0] = max(top[0], at)
            return made, at

        ((ident, Wq_hi, Wq_lo, Wvo, K_hi, K_lo, V_hi, V_lo, vscale, ffs, minus_half,
          nmax, den, rden, rden_wide, rden_row, stats, mv, ve, rstd), QO_AT) = lay(
            0, ("ident", [P, P], F),
            ("Wq_hi", [P, H, 2, P], R), ("Wq_lo", [P, H, 2, P], R),
            ("Wvo", [P, PAIRS, D], F),
            ("K_hi", [P, S], R), ("K_lo", [P, S], R),
            ("V_hi", [P, KT, KVR], F16), ("V_lo", [P, KT, KVR], F16),
            ("vscale", [P, 4], F),
            ("ffs", [P, 8], F),
            ("minus_half", [P, 4], F),
            ("nmax", [P, 4], F), ("den", [P, 2, 2, 4], F), ("rden", [P, 2, 2, 4], F),
            ("rden_wide", [P, 4, 2, KVR], F),
            ("rden_row", [P, HALF], F),
            ("stats", [P, QT, 6], F), ("mv", [P, QT, 2], F), ("ve", [P, QT], F), ("rstd", [P, QT], F))
        (QO,), HEAD_AT = lay(QO_AT, ("QO", [P, H, S], F))

        def rows_in(slot):
            return QO[:, slot:slot + 3:2, :].rearrange("p s (t d) -> p s t d", d=D)

        xr, res, x1, yo = rows_in(1), rows_in(5), rows_in(9), rows_in(13)

        def tok(rows, t):
            return rows[:, t // 4, t % 4, :]

        (Q_hi, Q_lo, probs), SHARED_AT = lay(
            HEAD_AT, ("Q_hi", [P, 2, S], R), ("Q_lo", [P, 2, S], R), ("probs", [P, 2, S], F))
        (TT,), _ = lay(HEAD_AT, ("TT", [P, W], R))
        (PT_hi, PT_lo), _ = lay(SHARED_AT, ("PT_hi", [P, 2, 2, KT, HALF], F16), ("PT_lo", [P, 2, 2, KT, HALF], F16))
        (xq, xT, tcos, tsin, wkv_raw, wkv, wdq, wdq_b), WORK_AT = lay(
            SHARED_AT, ("xq", [P, QT, D], F), ("xT", [P, KC, S], F), ("tcos", [P, S], F), ("tsin", [P, S], F),
            ("wkv_raw", [P, KC, P], F), ("wkv", [P, KC, P], F), ("wdq", [P, KC, QR], F),
            ("wdq_b", [P, KC, 2, QR - P], F))
        (cq_hi, cq_lo, cq_s), MUL_AT = lay(
            WORK_AT, ("cq_hi", [P, S], R), ("cq_lo", [P, S], R),
            ("cq_s", [P, S], R))
        (qmul,), _ = lay(MUL_AT, ("qmul", [P, 4, S], F))
        (Kf, kmul), _ = lay(MUL_AT, ("Kf", [P, S], F), ("kmul", [P, 2, S], F))
        (turned,), _ = lay(SHARED_AT, ("turned", [P, 2, S], F))
        (x1T_hi, x1T_lo, g_hi, g_lo), _ = lay(
            WORK_AT, ("x1T_hi", [P, KC, HALF], R), ("x1T_lo", [P, KC, HALF], R),
            ("g_hi", [P, HT, HALF], R), ("g_lo", [P, HT, HALF], R))
        act = QO[:, 0, :].rearrange("p (t q) -> p t q", t=2)
        gate = QO[:, 2, :].rearrange("p (t q) -> p t q", t=2)
        (wuq_a, wuq_b, wuk, wuv, wo, wqr), AT = lay(
            QO_AT, ("wuq_a", [P, H * DN], F), ("wuq_b", [QR - P, H * DN], F), ("wuk", [KVR, H * DN], F),
            ("wuv", [KVR, H * DV], F), ("wo", [P, H, D], F), ("wqr", [P, 2, H * DR], F))
        (ones, asum), AT = lay(AT, ("ones", [P, P], F), ("asum", [P, 4], F))
        assert AT <= HEAD_AT
        (tern,), AT = lay(HEAD_AT, ("tern", [P, W], R))
        (below,), AT = lay(AT, ("below", [P, HT * D], F))
        assert AT <= SHARED_AT
        (w13, w2n, wT, AT_sb), _ = lay(
            WORK_AT, ("w13", [P, 2, HT, D], F), ("w2n", [P, KC, HT * P], F), ("wT", [P, 2, QR + 2 * KVR], F),
            ("AT", [P, 2, 2, P], F))
        ff = (w13[:, 0, :, :].rearrange("p t d -> p (t d)"), w13[:, 1, :, :].rearrange("p t d -> p (t d)"),
              w2n[:, :, :].rearrange("p t h -> p (t h)"))
        assert top[0] <= 4 * arena.shape[1], (top[0], 4 * arena.shape[1])

        Sa = ctx.enter_context(nc.psum_tensor("Sa", [P, S], F))
        Sb = ctx.enter_context(nc.psum_tensor("Sb", [P, S], F))
        Ta = ctx.enter_context(nc.psum_tensor("Ta", [P, HALF], F))
        Tb = ctx.enter_context(nc.psum_tensor("Tb", [P, HALF], F))
        Oa = ctx.enter_context(nc.psum_tensor("Oa", [P, HALF], F))
        Ob = ctx.enter_context(nc.psum_tensor("Ob", [P, HALF], F))
        SS, TS, OS = (Sa, Sb), (Ta, Tb), (Oa, Ob)
        SQ = (Sa[:, 0:HALF], Sa[:, HALF:S], Sb[:, 0:HALF], Sb[:, HALF:S])
        FF = (SQ[2], SQ[3], Ta[:, :], Tb[:, :])

        held = sem("held")
        const_ready = sem("const_ready")
        w_qk_in = (sem("w_qk_in0"), sem("w_qk_in1"))
        w_o_in = (sem("w_o_in0"), sem("w_o_in1"), sem("w_o_in2"))
        w_qr_in, w_ff_in = sem("w_qr_in"), sem("w_ff_in")
        pad_ready = sem("pad_ready")
        wt_ps, wt_sb = sem("wt_ps"), sem("wt_sb")
        prod_ps, at_sb, wvo_sb, back_ps = sem("prod_ps"), sem("at_sb"), sem("wvo_sb"), sem("back_ps")
        prod_hi, prod_lo = sem("prod_hi"), sem("prod_lo")
        qr_hi, qr_lo = sem("qr_hi"), sem("qr_lo")
        ff_sum, abs_done, ff_mean, ff_step = sem("ff_sum"), sem("abs_done"), sem("ff_mean"), sem("ff_step")
        ff_tern, ff_ps, ff_sb, ff_out = sem("ff_tern"), sem("ff_ps"), sem("ff_sb"), sem("ff_out")
        proj_in = sem("proj_in")
        w_small = sem("w_small")
        xT_ps, xT_sb = sem("xT_ps"), sem("xT_sb")
        kv_ps, cqa_ps, cqb_ps = sem("kv_ps"), sem("cqa_ps"), sem("cqb_ps")
        k_lat, k_step, k_hi = sem("k_lat"), sem("k_step"), sem("k_hi")
        v_ps, v_hi = sem("v_ps"), sem("v_hi")
        cq_hid, cq_lod = sem("cq_hid"), sem("cq_lod")
        q_ps, rope_mul, rope_sum, lat_out = sem("q_ps"), sem("rope_mul"), sem("rope_sum"), sem("lat_out")
        turned_out = (sem("even_out"), sem("odd_out"))
        q_split_hi, q_split_lo = sem("q_split_hi"), sem("q_split_lo")
        scores_ready, max_ready, exp_done = sem("scores_ready"), sem("max_ready"), sem("exp_done")
        pt_ps, pt_hi, pt_lo = sem("pt_ps"), sem("pt_hi"), sem("pt_lo")
        pv_done, rden_ready, row_ps, row_ready = sem("pv_done"), sem("rden_ready"), sem("row_ps"), sem("row_ready")
        wide_ready = sem("wide_ready")
        out_ready = sem("out_ready")
        xr_in, tt_in = sem("xr_in"), sem("tt_in")
        att_ps, att_res, ln_step, ln_pow = sem("att_ps"), sem("att_res"), sem("ln_step"), sem("ln_pow")
        x1_ready, x1T_ps, x1T_hid, x1T_lod = sem("x1_ready"), sem("x1T_ps"), sem("x1T_hid"), sem("x1T_lod")
        h_ps, silu_done, gate_done = sem("h_ps"), sem("silu_done"), sem("gate_done")
        ghi_done, glo_done, y_ps, y_res = sem("ghi_done"), sem("glo_done"), sem("y_ps"), sem("y_res")
        y_ready, y_out, y_stored = sem("y_ready"), sem("y_out"), sem("y_stored")

        block = ctx.enter_context(nc.Block())

        def hold(eng, s, value):
            eng.wait_ge(s, value)
            eng.sem_inc(held, 1)

        @block.sync
        def _(sp):
            def absorbed_weights(part, heads):
                cols = slice(heads[0] * DN, heads[1] * DN)
                sp.dma_start(wuq_a[:, cols], w_uq[0:P, cols]).then_inc(w_qk_in[part], 16)
                sp.dma_start(wuq_b[:, cols], w_uq[P:QR, cols]).then_inc(w_qk_in[part], 16)
                sp.dma_start(wuk[:, cols], w_uk[:, cols]).then_inc(w_qk_in[part], 16)
                sp.dma_start(wuv[:, cols], w_uv[:, cols]).then_inc(w_qk_in[part], 16)

            def output_weights(part, heads):
                sp.dma_start(wo[:, heads[0]:heads[1], :], wo_v[:, heads[0]:heads[1], :]).then_inc(w_o_in[part], 16)

            absorbed_weights(0, (0, 4))
            output_weights(0, (0, 4))
            absorbed_weights(1, (4, H))
            output_weights(1, (4, 8))
            output_weights(2, (8, H))
            sp.wait_ge(pad_ready, 3)
            for i, w in enumerate((w1, w3)):
                sp.dma_start(w13[:, i, 0:HT - 1, :],
                             w[0:(HT - 1) * P, :].rearrange("(t p) d -> p t d", p=P)).then_inc(w_ff_in, 16)
                sp.dma_start(w13[0:LAST, i, HT - 1, :], w[(HT - 1) * P:HID, :]).then_inc(w_ff_in, 16)
            sp.dma_start(w2n[:, :, 0:HID], w2.rearrange("(t p) h -> p t h", p=P)).then_inc(w_ff_in, 16)
            sp.dma_start(wqr[:, 0, :], w_qr[0:P, :]).then_inc(w_qr_in, 16)
            sp.dma_start(wqr[0:64, 1, :], w_qr[P:QR, :]).then_inc(w_qr_in, 16)
            sp.dma_start(wqr[64:128, 1, :], w_qr[P:QR, :]).then_inc(w_qr_in, 16)

            with sp.Fori(0, B) as b:
                sp.wait_ge(pv_done, b * 2 * PAIRS + PV0)
                sp.dma_start(xq[:, :, :], x_v[b]).then_inc(proj_in, 16)
                for kc in range(KC):
                    sp.dma_start(wkv_raw[:, kc, 0:DR], w_kr[kc * P:(kc + 1) * P, :]).then_inc(proj_in, 16)
                    sp.dma_start(wkv_raw[:, kc, DR:P], w_dkv[kc * P:(kc + 1) * P, :]).then_inc(proj_in, 16)
                    sp.dma_start(wdq[:, kc, :], w_dq[kc * P:(kc + 1) * P, :]).then_inc(proj_in, 16)
                sp.dma_start(tcos[:, :], cos).then_inc(proj_in, 16)
                sp.dma_start(tsin[:, :], sin).then_inc(proj_in, 16)
                for g in range(GROUPS):
                    if g == 1:
                        hold(sp, y_ready, b * 2 + Y0)
                    if g == 3:
                        hold(sp, y_stored, b + STORED0)
                    for j in range(2):
                        sp.wait_ge(rope_sum, b * 2 * GROUPS + 2 * g + j + 1)
                        for s in range(4):
                            sp.dma_start(QO[32 * j:32 * j + 32, 4 * g + s, :],
                                         turned[32 * s:32 * s + 32, j, :]).then_inc(turned_out[j], 16)
                sp.wait_ge(q_split_lo, b * H + 4)
                for h in range(2):
                    sp.dma_start(xr[:, h, :, :], x_v[b][:, 4 * h:4 * h + 4, :]).then_inc(xr_in, 16)
                sp.wait_ge(ff_out, 16)
                sp.wait_ge(pt_ps, b * 2 * TILES * PAIRS + 2 * TILES * PAIRS + PT0)
                sp.dma_start(TT[:, :].bitcast(F), ternary).then_inc(tt_in, 16)

        @block.gpsimd
        def _(pool):
            nc.gpsimd.memset(ident[:, :], 0.0).then_inc(const_ready, 1)
            nc.gpsimd.memset(ones[:, :], 1.0).then_inc(const_ready, 1)
            nc.gpsimd.memset(minus_half[:, :], -0.5).then_inc(const_ready, 1)
            pool.wait_ge(const_ready, 3)
            nc.gpsimd.affine_select(out=ident[:, :], in_=ident[:, :], compare_op=ALU.not_equal, fill=1.0, base=0,
                                    pattern=[[-1, P]], channel_multiplier=1).then_inc(const_ready, 1)
            for i in range(2):
                nc.gpsimd.memset(w13[:, i, HT - 1, :], 0.0).then_inc(pad_ready, 1)
            nc.gpsimd.memset(w2n[:, :, HID:HT * P], 0.0).then_inc(pad_ready, 1)
            pool.sem_inc(y_stored, STORED0)

            with pool.Fori(0, B) as b:
                def split_low(tile, pair, a):
                    pool.wait_ge(q_split_hi, pair * 2 + a + 1)
                    nc.gpsimd.tensor_tensor(Q_lo[:, a, :], QO[:, tile, :], Q_hi[:, a, :].bitcast(F),
                                            ALU.subtract).then_inc(q_split_lo, 1)

                for g in range(GROUPS):
                    for j, op in enumerate((ALU.subtract, ALU.add)):
                        pool.wait_ge(rope_mul, b * 4 * GROUPS + 4 * g + j + 3)
                        if g >= 1:
                            pool.wait_ge(turned_out[j], b * 64 * GROUPS + 64 * g)
                        nc.gpsimd.tensor_tensor(turned[:, j, :], qmul[:, 2 * j, :], qmul[:, 2 * j + 1, :],
                                                op).then_inc(rope_sum, 1)
                    if g == 1:
                        for a in range(2):
                            split_low(a, b * PAIRS, a)

                def widen(group, h):
                    hold(pool, rden_ready, group + 1)
                    src = rden[:, h].rearrange("p a t -> p t a").unsqueeze(3).broadcast_to([P, 4, 2, KVR])
                    nc.gpsimd.tensor_scalar(rden_wide[:, :, :, :], src, 1.0, 1.0, ALU.mult,
                                            ALU.mult).then_inc(wide_ready, 1)

                def pair_pool(p, first, last):
                    pair = b * PAIRS + p
                    if not first:
                        widen(pair * 2 - 1, 1)
                    widen(pair * 2, 0)
                    if not last:
                        for a in range(2):
                            split_low(p * 2 + 2 + a, pair + 1, a)

                pair_pool(0, True, False)
                with pool.Fori(1, PAIRS - 1) as p:
                    pair_pool(p, False, False)
                pair_pool(PAIRS - 1, False, True)
                widen(b * PAIRS * 2 + 2 * PAIRS - 1, 1)

                def power(h, n):
                    pool.wait_ge(ln_step, n)
                    nc.gpsimd.tensor_tensor(rstd[:, 4 * h:4 * h + 4], ve[:, 4 * h:4 * h + 4], minus_half[:, :],
                                            ALU.pow).then_inc(ln_pow, 1)

                for h in range(2):
                    power(h, b * 4 + h + 1)
                for h in range(2):
                    for t in range(HT):
                        pool.wait_ge(ghi_done, b * 2 * HT + HT * h + t + 1)
                        nc.gpsimd.tensor_tensor(g_lo[:, t, :], gate[:, t % 2, :], g_hi[:, t, :].bitcast(F),
                                                ALU.subtract).then_inc(glo_done, 1)
                    power(h, b * 4 + 3 + h)
                    pool.wait_ge(y_ready, b * 2 + h + 1 + Y0)
                    nc.gpsimd.dma_start(out_v[b][:, 4 * h:4 * h + 4, :], yo[:, h, :, :]).then_inc(y_out, 16)
                pool.wait_ge(y_out, b * 32 + 32)
                pool.sem_inc(y_stored, 1)

        @block.scalar
        def _(act_):
            def copy(o, i, scale=1.0):
                return nc.scalar.activation(o, i, ACT.Copy, scale=scale)

            act_.sem_inc(exp_done, EXP0)
            act_.sem_inc(row_ready, ROW0)

            def weights_out(h):
                act_.wait_ge(wt_ps, h + 1)
                if h >= 2:
                    act_.wait_ge(prod_ps, h - 1)
                copy(wT[:, h % 2, :], TS[h % 2][:, 0:QR + 2 * KVR]).then_inc(wt_sb, 1)

            def products_out(j):
                act_.wait_ge(prod_ps, 2 * j + 2)
                if j >= 2:
                    act_.wait_ge(back_ps, j - 1)
                bank = OS[j % 2]
                copy(AT_sb[:, j % 2, 0, :], bank[:, 0:P])
                copy(AT_sb[:, j % 2, 1, :].rearrange("p (c r) -> p c r", c=2),
                     bank[:, P:QR].unsqueeze(1).broadcast_to([P, 2, QR - P])).then_inc(at_sb, 1)

            def product_high(j):
                act_.wait_ge(back_ps, j + 1)
                tile = 4 * (j // 2) + 2 + j % 2
                copy(Wq_hi[:, tile, :, :], SQ[j % 2][:, 0:256].rearrange("p (c m) -> p c m", c=2)).then_inc(prod_hi, 1)

            def absolute_sum(i):
                act_.wait_ge(w_ff_in, 80)
                act_.wait_ge(pad_ready, 3)
                if i == 2:
                    act_.wait_ge(abs_done, 1)
                nc.scalar.activation(below[:, :], ff[i], ACT.Abs, accum_out=asum[:, i:i + 1]).then_inc(abs_done, 1)

            def rotary_high(j, c):
                act_.wait_ge(w_qr_in, 48)
                src = wqr[:, c, :].rearrange("p (g m two) -> p two g m", two=2, m=P)[:, j]
                copy(Wq_hi[:, j::4, c, :], src).then_inc(qr_hi, 1)

            weights_out(0)
            weights_out(1)
            for h in range(H):
                if h % 2:
                    products_out(h // 2)
                elif h:
                    product_high(h // 2 - 1)
                if h in (9, 10):
                    absolute_sum(h - 8)
                if h >= 12:
                    rotary_high((h - 12) // 2, h % 2)
                if h + 2 < H:
                    weights_out(h + 2)
            product_high(PAIRS - 1)
            for n in range(9):
                act_.wait_ge(ff_ps, n + 1)
                copy(tern[:, n * HALF:(n + 1) * HALF], FF[n % 4]).then_inc(ff_sb, 1)
            act_.wait_ge(ff_sb, 9)
            act_.dma_start(ternary, tern[:, :].bitcast(F)).then_inc(ff_out, 16)

            with act_.Fori(0, B) as b:
                for n in range(4):
                    act_.wait_ge(xT_ps, b * 4 + n + 1)
                    copy(xT[:, n % 2, n // 2 * HALF:(n // 2 + 1) * HALF], (Ta, Tb, Oa, Ob)[n][:, :]).then_inc(xT_sb, 1)
                act_.wait_ge(kv_ps, b + 1)
                copy(Kf[64:128, :], Sa[64:128, :]).then_inc(k_lat, 1)
                act_.wait_ge(cqa_ps, b + 1)
                copy(cq_hi[:, :], Sb[:, :], SCALE).then_inc(cq_hid, 1)
                act_.wait_ge(cqb_ps, b + 1)
                for n in range(2):
                    copy(cq_s[:, n * HALF:(n + 1) * HALF], TS[n][:, :], SCALE).then_inc(cq_hid, 1)
                act_.wait_ge(k_lat, b + 1)
                act_.wait_ge(k_step, b * 11 + 4)
                copy(K_hi[:, :], Kf[:, :]).then_inc(k_hi, 1)
                act_.wait_ge(v_ps, b + 1)
                copy(V_hi[:, :, :], Oa[:, :].rearrange("p (k c) -> p k c", k=KT)).then_inc(v_hi, 1)
                def split_high(tile, pair, a, free):
                    if free is not None:
                        act_.wait_ge(scores_ready, free)
                    copy(Q_hi[:, a, :], QO[:, tile, :]).then_inc(q_split_hi, 1)

                for g in range(GROUPS):
                    if g == 1:
                        act_.wait_ge(y_ready, b * 2 + Y0)
                    if g == 3:
                        act_.wait_ge(y_stored, b + STORED0)
                    for i in range(2):
                        act_.wait_ge(q_ps, b * 4 * GROUPS + 4 * g + 3 + i)
                        for n in range(2):
                            for a in range(2):
                                bank = (TS, OS)[i][n]
                                copy(QO[64:128, 4 * g + 2 * i + a, n * HALF:(n + 1) * HALF],
                                     bank[64 * a:64 * a + 64, :]).then_inc(lat_out, 1)
                    if g == 1:
                        act_.wait_ge(ff_out, 16)
                        act_.wait_ge(lat_out, b * 8 * GROUPS + 8)
                        for j in range(2):
                            act_.wait_ge(turned_out[j], b * 64 * GROUPS + 64)
                        for a in range(2):
                            split_high(a, b * PAIRS, a, None)

                def exponent(tile, n):
                    act_.wait_ge(max_ready, tile + 1)
                    act_.wait_ge(pt_ps, tile * 2 + 2)
                    nc.scalar.activation(probs[:, n % 2, :], SS[n % 2][:, :], ACT.Exp, bias=nmax[:, n % 4:n % 4 + 1],
                                         accum_out=den[:, n // 8 % 2, n // 4 % 2, n % 4:n % 4 + 1]).then_inc(exp_done, 1)

                def transposed_high(tile, n):
                    for j in range(2):
                        act_.wait_ge(pt_ps, PT0 + tile * 2 + j + 1)
                        dst = PT_hi[:, 1 - n // 8, n // 4 % 2, 4 * j:4 * j + 4, n % 4 * P:n % 4 * P + P]
                        copy(dst, TS[j][:, :].rearrange("p (k q) -> p k q", k=4), PROB_UP).then_inc(pt_hi, 1)

                def row_out(group):
                    act_.wait_ge(row_ps, group + 1)
                    act_.wait_ge(out_ready, group + 1)
                    copy(rden_row[:, :], Ob[:, :]).then_inc(row_ready, 1)

                def pair_act(p, first, last):
                    pair = b * PAIRS + p
                    t0 = pair * TILES
                    for n in range(TILES):
                        if not (last and n == TILES - 1):
                            exponent(t0 + n + 1, n + 1)
                        if first and n == 8:
                            act_.wait_ge(lat_out, b * 8 * GROUPS + 8 * GROUPS)
                            for j in range(2):
                                act_.wait_ge(turned_out[j], b * 64 * GROUPS + 64 * GROUPS)
                        transposed_high(t0 + n, n)
                        if n in (3, 11) and not (first and n == 3):
                            row_out(pair * 2 + (n // 8) - 1)
                        if n in (10, 14) and not last:
                            split_high(p * 2 + 2 + n // 12, pair + 1, n // 12, t0 + (12 if n == 10 else 16))

                exponent(b * PAIRS * TILES, 0)
                pair_act(0, True, False)
                with act_.Fori(1, PAIRS - 1) as p:
                    pair_act(p, False, False)
                pair_act(PAIRS - 1, False, True)
                row_out(b * PAIRS * 2 + 2 * PAIRS - 1)

                def x1_high(h):
                    act_.wait_ge(x1T_ps, b * 2 + h + 1)
                    for c in range(KC):
                        copy(x1T_hi[:, c, :], TS[c][:, :]).then_inc(x1T_hid, 1)

                for h in range(2):
                    x1_high(h)
                    for t in range(HT):
                        u = b * 2 * HT + HT * h + t
                        act_.wait_ge(h_ps, u + 1)
                        if HT * h + t >= 2:
                            act_.wait_ge(gate_done, u - 1)
                        bank = (Oa[:, :], Sa[:, 0:HALF])[t % 2]
                        nc.scalar.activation(act[:, t % 2, :], bank, ACT.Silu, scale=ffs[:, 0:1]).then_inc(silu_done, 1)
                        act_.wait_ge(gate_done, u + 1)
                        if h == 1 and t == 0:
                            act_.wait_ge(y_ps, b * 8 + 4)
                        copy(g_hi[:, t, :], gate[:, t % 2, :]).then_inc(ghi_done, 1)

        @block.vector
        def _(dve):
            dve.sem_inc(pt_lo, LO0)
            dve.sem_inc(out_ready, OUT0)
            dve.sem_inc(y_ready, Y0)

            def product_low(j):
                dve.wait_ge(at_sb, j + 1)
                nc.vector.tensor_copy(Wvo[:, j, :], OS[j % 2][:, 256:512]).then_inc(wvo_sb, 1)
                dve.wait_ge(prod_hi, j + 1)
                tile = 4 * (j // 2) + 2 + j % 2
                nc.vector.tensor_tensor(Wq_lo[:, tile, :, :], SQ[j % 2][:, 0:256].rearrange("p (c m) -> p c m", c=2),
                                        Wq_hi[:, tile, :, :].bitcast(F), ALU.subtract).then_inc(prod_lo, 1)

            def ternary_scales():
                dve.wait_ge(ff_mean, 1)
                nc.vector.tensor_scalar(ffs[:, 0:3], Sb[:, 0:3], 1.0 / (HID * D), None, ALU.mult).then_inc(ff_step, 1)
                dve.wait_ge(ff_step, 1)
                nc.vector.tensor_scalar(ffs[:, 3:6], ffs[:, 0:3], 0.5, None, ALU.mult).then_inc(ff_step, 1)
                nc.vector.tensor_tensor(ffs[:, 6:7], ffs[:, 1:2], ffs[:, 2:3], ALU.mult).then_inc(ff_step, 1)
                dve.wait_ge(ff_step, 3)

            def ternary_weight(i):
                if i:
                    dve.wait_ge(ff_tern, i)
                nc.vector.tensor_scalar(below[:, :], ff[i], -1.0, ffs[:, 3 + i:4 + i], ALU.mult, ALU.is_gt).then_inc(ff_step, 1)
                dve.wait_ge(ff_step, 4 + i)
                nc.vector.scalar_tensor_tensor(ff[i], ff[i], ffs[:, 3 + i:4 + i], below[:, :], ALU.is_gt,
                                               ALU.subtract).then_inc(ff_tern, 1)

            for j in range(PAIRS):
                product_low(j)
                if j == 3:
                    dve.wait_ge(w_ff_in, 80)
                    dve.wait_ge(pad_ready, 3)
                    nc.vector.tensor_reduce(asum[:, 0:1], ff[0], AX.X, ALU.add,
                                            apply_absolute_value=True).then_inc(ff_sum, 1)
                if j == 5:
                    ternary_scales()
                if j >= 5:
                    ternary_weight(j - 5)
            for j in range(2):
                for c in range(2):
                    dve.wait_ge(qr_hi, 2 * j + c + 1)
                    src = wqr[:, c, :].rearrange("p (g m two) -> p two g m", two=2, m=P)[:, j]
                    nc.vector.tensor_tensor(Wq_lo[:, j::4, c, :], src, Wq_hi[:, j::4, c, :].bitcast(F),
                                            ALU.subtract).then_inc(qr_lo, 1)

            with dve.Fori(0, B) as b:
                dve.wait_ge(proj_in, b * 144 + 144)
                nc.vector.tensor_copy(wkv[:, :, 0:DR].rearrange("p c (two i) -> p c two i", two=2),
                                      wkv_raw[:, :, 0:DR].rearrange("p c (i two) -> p c two i", two=2)).then_inc(w_small, 1)
                nc.vector.tensor_copy(wkv[:, :, DR:P], wkv_raw[:, :, DR:P]).then_inc(w_small, 1)
                for a in range(2):
                    nc.vector.tensor_copy(wdq_b[:, :, a, :], wdq[:, :, P:QR]).then_inc(w_small, 1)

                K0 = b * 11
                dve.wait_ge(kv_ps, b + 1)
                nc.vector.tensor_tensor(kmul[0:64, 0, :], Sa[0:64, :], tcos[0:64, :], ALU.mult)
                nc.vector.tensor_tensor(kmul[32:64, 1, :], Sa[0:32, :], tsin[0:32, :], ALU.mult).then_inc(k_step, 1)
                nc.vector.tensor_tensor(kmul[0:32, 1, :], Sa[32:64, :], tsin[32:64, :], ALU.mult).then_inc(k_step, 1)
                dve.wait_ge(k_step, K0 + 2)
                nc.vector.tensor_tensor(Kf[0:32, :], kmul[0:32, 0, :], kmul[0:32, 1, :], ALU.subtract).then_inc(k_step, 1)
                nc.vector.tensor_tensor(Kf[32:64, :], kmul[32:64, 0, :], kmul[32:64, 1, :], ALU.add).then_inc(k_step, 1)
                dve.wait_ge(cq_hid, b * 3 + 1)
                nc.vector.scalar_tensor_tensor(cq_lo[:, :], Sb[:, :], SCALE, cq_hi[:, :].bitcast(F), ALU.mult,
                                               ALU.subtract).then_inc(cq_lod, 1)
                dve.wait_ge(cq_hid, b * 3 + 3)
                for n in range(2):
                    low = cq_s[64:128, n * HALF:(n + 1) * HALF]
                    nc.vector.scalar_tensor_tensor(low, TS[n][64:128, :], SCALE, low.bitcast(F), ALU.mult,
                                                   ALU.subtract).then_inc(cq_lod, 1)
                dve.wait_ge(k_lat, b + 1)
                nc.vector.tensor_reduce(vscale[64:128, 0:1], Kf[64:128, :], AX.X, ALU.max,
                                        apply_absolute_value=True).then_inc(k_step, 1)
                dve.wait_ge(k_step, K0 + 5)
                nc.vector.tensor_scalar(vscale[64:128, 1:2], vscale[64:128, 0:1], 1e-30, None, ALU.max).then_inc(k_step, 1)
                dve.wait_ge(k_step, K0 + 6)
                nc.vector.tensor_scalar(vscale[64:128, 0:1].bitcast(I32), vscale[64:128, 1:2].bitcast(I32),
                                        0x7F800000, None, ALU.bitwise_and).then_inc(k_step, 1)
                dve.wait_ge(k_step, K0 + 7)
                nc.vector.reciprocal(vscale[64:128, 2:3], vscale[64:128, 0:1]).then_inc(k_step, 1)
                nc.vector.tensor_scalar(vscale[64:128, 3:4], vscale[64:128, 0:1], 1.0 / (PROB_UP * VAL_UP), None,
                                        ALU.mult).then_inc(k_step, 1)
                dve.wait_ge(k_step, K0 + 9)
                nc.vector.tensor_copy(vscale[0:64, 3:4], vscale[64:128, 3:4])
                nc.vector.tensor_scalar(kmul[64:128, 0, :], Kf[64:128, :], vscale[64:128, 2:3], VAL_UP, ALU.mult,
                                        ALU.mult).then_inc(k_step, 1)
                dve.wait_ge(k_hi, b + 1)
                nc.vector.tensor_tensor(K_lo[:, :], Kf[:, :], K_hi[:, :].bitcast(F), ALU.subtract).then_inc(k_step, 1)
                dve.wait_ge(v_hi, b + 1)
                nc.vector.tensor_tensor(V_lo[:, :, :], Oa[:, :].rearrange("p (k c) -> p k c", k=KT), V_hi[:, :, :],
                                        ALU.subtract).then_inc(cq_lod, 1)
                dve.wait_ge(k_step, K0 + 11)
                for g in range(GROUPS):
                    for j, (tile, table, dst) in enumerate(((0, tcos, 0), (0, tsin, 2), (1, tsin, 1), (1, tcos, 3))):
                        if tile == j // 2 and j % 2 == 0:
                            dve.wait_ge(q_ps, b * 4 * GROUPS + 4 * g + tile + 1)
                        if g >= 1:
                            dve.wait_ge(rope_sum, b * 2 * GROUPS + 2 * g - 1 + dst // 2)
                        nc.vector.tensor_tensor(qmul[:, dst, :], SS[tile][:, :], table[:, :], ALU.mult).then_inc(rope_mul, 1)

                def maximum(tile, n):
                    dve.wait_ge(scores_ready, tile + 1)
                    nc.vector.tensor_reduce(nmax[:, n % 4:n % 4 + 1], SS[n % 2][:, :], AX.X, ALU.max,
                                            negate=True).then_inc(max_ready, 1)

                def transposed_low(tile, n):
                    for j in range(2):
                        dve.wait_ge(pt_hi, tile * 2 + j + 1)
                        place = (slice(None), 1 - n // 8, n // 4 % 2, slice(4 * j, 4 * j + 4), slice(n % 4 * P, n % 4 * P + P))
                        nc.vector.scalar_tensor_tensor(PT_lo[place], TS[j][:, :].rearrange("p (k q) -> p k q", k=4),
                                                       PROB_UP, PT_hi[place], ALU.mult, ALU.subtract).then_inc(pt_lo, 1)

                def reciprocal(group, h):
                    dve.wait_ge(exp_done, EXP0 + group * 8 + 8)
                    nc.vector.reciprocal(rden[:, h], den[:, h]).then_inc(rden_ready, 1)

                def normalise(group, pair_row, h):
                    dve.wait_ge(pv_done, PV0 + group + 1)
                    dve.wait_ge(row_ready, ROW0 + group + 1)
                    nc.vector.scalar_tensor_tensor(QO[:, pair_row, h * HALF:(h + 1) * HALF], Oa[:, :], vscale[:, 3:4],
                                                   rden_row[:, :], ALU.mult, ALU.mult).then_inc(out_ready, 1)

                def pair_dve(p, first, last):
                    pair = b * PAIRS + p
                    t0 = pair * TILES
                    for n in range(TILES):
                        h = n // 8
                        if n % 8 == 0:
                            if not first:
                                normalise(pair * 2 + h - 2, p * 2 - 2, h)
                            if not (first and h == 0):
                                reciprocal(pair * 2 + h - 1, 1 - h)
                        if not (last and n >= TILES - 2):
                            maximum(t0 + n + 2, n + 2)
                        transposed_low(t0 + n, n)

                for n in range(2):
                    maximum(b * PAIRS * TILES + n, n)
                dve.wait_ge(rope_sum, b * 2 * GROUPS + 2 * GROUPS)
                pair_dve(0, True, False)
                with dve.Fori(1, PAIRS - 1) as p:
                    pair_dve(p, False, False)
                pair_dve(PAIRS - 1, False, True)
                group = b * PAIRS * 2 + 2 * PAIRS
                normalise(group - 2, 2 * PAIRS - 2, 0)
                reciprocal(group - 1, 1)

                def statistics(t, n):
                    nc.vector.bn_stats(stats[:, t, :], tok(res, t)).then_inc(att_res, 1)
                    hold(dve, att_res, n + 2)
                    nc.vector.bn_aggr(mv[:, t, :], stats[:, t, :]).then_inc(att_res, 1)

                def add_eps(h, n):
                    dve.wait_ge(att_res, n)
                    nc.vector.tensor_scalar(ve[:, 4 * h:4 * h + 4], mv[:, 4 * h:4 * h + 4, 1], EPS, None,
                                            ALU.add).then_inc(ln_step, 1)

                A0 = b * 48

                def attention_rows(h):
                    for t in range(4 * h, 4 * h + 4):
                        dve.wait_ge(att_ps, b * 8 + t + 1)
                        nc.vector.tensor_tensor(tok(res, t), SQ[t % 4][:, 0:D], tok(xr, t), ALU.add).then_inc(att_res, 1)
                        dve.wait_ge(att_res, A0 + 3 * t + 1)
                        statistics(t, A0 + 3 * t)
                    add_eps(h, A0 + 12 * h + 12)

                def first_norm(h):
                    dve.wait_ge(ln_pow, b * 4 + h + 1)
                    for t in range(4 * h, 4 * h + 4):
                        nc.vector.tensor_scalar(tok(x1, t), tok(res, t), mv[:, t, 0:1], rstd[:, t:t + 1],
                                                ALU.subtract, ALU.mult).then_inc(x1_ready, 1)

                dve.wait_ge(xr_in, b * 32 + 32)
                attention_rows(0)
                first_norm(0)
                normalise(group - 1, 2 * PAIRS - 2, 1)

                def x1_low(h):
                    for c in range(KC):
                        dve.wait_ge(x1T_hid, b * 4 + 2 * h + c + 1)
                        nc.vector.tensor_tensor(x1T_lo[:, c, :], TS[c][:, :], x1T_hi[:, c, :].bitcast(F),
                                                ALU.subtract).then_inc(x1T_lod, 1)

                def gates(h):
                    for t in range(HT):
                        u = b * 2 * HT + HT * h + t
                        dve.wait_ge(silu_done, u + 1)
                        if HT * h + t >= 2:
                            dve.wait_ge(glo_done, u - 1)
                        bank = (Ob[:, :], Sa[:, HALF:S])[t % 2]
                        nc.vector.tensor_tensor(gate[:, t % 2, :], bank, act[:, t % 2, :], ALU.mult).then_inc(gate_done, 1)

                def results(h):
                    for t in range(4 * h, 4 * h + 4):
                        n = A0 + 24 + 3 * t
                        dve.wait_ge(y_ps, b * 8 + t + 1)
                        nc.vector.scalar_tensor_tensor(tok(res, t), SQ[2 + t % 2][:, 0:D], ffs[:, 6:7],
                                                       tok(x1, t), ALU.mult, ALU.add).then_inc(att_res, 1)
                        dve.wait_ge(att_res, n + 1)
                        statistics(t, n)
                    add_eps(h, A0 + 24 + 12 * h + 12)
                    dve.wait_ge(ln_pow, b * 4 + 3 + h)
                    for t in range(4 * h, 4 * h + 4):
                        last = nc.vector.tensor_scalar(tok(yo, t), tok(res, t), mv[:, t, 0:1], rstd[:, t:t + 1],
                                                       ALU.subtract, ALU.mult)
                    last.then_inc(y_ready, 1)

                x1_low(0)
                attention_rows(1)
                first_norm(1)
                gates(0)
                x1_low(1)
                results(0)
                gates(1)
                results(1)

        @block.tensor
        def _(pe):
            mm = nc.tensor.matmul
            pe.sem_inc(pt_ps, PT0)
            pe.sem_inc(pv_done, PV0)

            pe.wait_ge(const_ready, 4)

            def turn_weights(h):
                if h in (0, 4):
                    pe.wait_ge(w_qk_in[h // 4], 64)
                if h >= 2:
                    pe.wait_ge(wt_sb, h - 1)
                bank, cols = TS[h % 2], slice(h * DN, (h + 1) * DN)
                nc.tensor.transpose(bank[:, 0:128], wuq_a[:, cols], ident[:, :])
                nc.tensor.transpose(bank[:, 128:192], wuq_b[:, cols], ident[0:64, 0:64])
                nc.tensor.transpose(bank[:, 192:256], wuk[:, cols], ident[0:64, 0:64])
                nc.tensor.transpose(bank[:, 256:320], wuv[:, cols], ident[0:64, 0:64]).then_inc(wt_ps, 1)

            def weight_products(h):
                if h in (0, 4, 8):
                    pe.wait_ge(w_o_in[h // 4], 16)
                pe.wait_ge(wt_sb, h + 1)
                j, a = h // 2, h % 2
                if a == 0 and j >= 2:
                    pe.wait_ge(at_sb, j - 1)
                    pe.wait_ge(wvo_sb, j - 1)
                w, bank = wT[:, a, :], OS[j % 2]
                mm(bank[64 * a:64 * a + 64, 0:QR], w[:, 192:256], w[:, 0:QR], start=True, stop=True)
                mm(bank[64 * a:64 * a + 64, 256:512], w[:, 256:320], wo[:, h, :], start=True, stop=True).then_inc(prod_ps, 1)

            def turn_products(j):
                pe.wait_ge(at_sb, j + 1)
                if j >= 2:
                    pe.wait_ge(prod_lo, j - 1)
                nc.tensor.transpose(SQ[j % 2][:, 0:P], AT_sb[:, j % 2, 0, :], ident[:, :])
                nc.tensor.transpose(SQ[j % 2][:, P:2 * P], AT_sb[:, j % 2, 1, :], ident[:, :]).then_inc(back_ps, 1)

            def turn_ternary(n):
                pe.wait_ge(ff_tern, n // 3 + 1)
                if n >= 4:
                    pe.wait_ge(ff_sb, n - 3)
                for k in range(4):
                    i = 4 * (n % 3) + k
                    if n < 6:
                        src = w13[:, n // 3, i % HT, i // HT * P:i // HT * P + P]
                    else:
                        src = w2n[:, i % KC, i // KC * P:i // KC * P + P]
                    last = nc.tensor.transpose(FF[n % 4][:, k * P:(k + 1) * P], src, ident[:, :])
                last.then_inc(ff_ps, 1)

            turn_weights(0)
            turn_weights(1)
            for h in range(H):
                weight_products(h)
                if h == 12:
                    pe.wait_ge(ff_sum, 1)
                    pe.wait_ge(abs_done, 2)
                    mm(Sb[:, 0:3], ones[:, :], asum[:, 0:3], start=True, stop=True).then_inc(ff_mean, 1)
                if h % 2 == 0 and h:
                    turn_products(h // 2 - 1)
                if h + 2 < H:
                    turn_weights(h + 2)
            turn_products(PAIRS - 1)
            for n in range(9):
                turn_ternary(n)
            pe.wait_ge(ff_sb, 8)

            with pe.Fori(0, B) as b:
                pe.wait_ge(proj_in, b * 144 + 144)
                for n in range(4):
                    for t in range(4):
                        last = nc.tensor.transpose((Ta, Tb, Oa, Ob)[n][:, t * P:(t + 1) * P],
                                                   xq[:, n // 2 * 4 + t, n % 2 * P:n % 2 * P + P], ident[:, :])
                    last.then_inc(xT_ps, 1)
                pe.wait_ge(w_small, b * 4 + 4)

                def project(outs, lhs, signal):
                    for n in range(2):
                        if signal is kv_ps:
                            pe.wait_ge(xT_sb, b * 4 + 2 * n + 2)
                        for kc in range(KC):
                            last = mm(outs[n], lhs(kc), xT[:, kc, n * HALF:(n + 1) * HALF],
                                      start=(kc == 0), stop=(kc == KC - 1))
                    last.then_inc(signal, 1)

                project((Sa[:, 0:HALF], Sa[:, HALF:S]), lambda kc: wkv[:, kc, :], kv_ps)
                pe.wait_ge(ff_sb, 9)
                pe.wait_ge(y_ready, b * 2 + Y0)
                project((Sb[:, 0:HALF], Sb[:, HALF:S]), lambda kc: wdq[:, kc, 0:P], cqa_ps)
                project((Ta[:, :], Tb[:, :]), lambda kc: wdq_b[:, kc, :, :], cqb_ps)

                def turn_values():
                    hold(pe, k_step, b * 11 + 10)
                    for k in range(KT):
                        last = nc.tensor.transpose(Oa[:, k * KVR:(k + 1) * KVR], kmul[64:128, 0, k * P:(k + 1) * P],
                                                   ident[64:128, 64:128])
                    last.then_inc(v_ps, 1)

                pe.wait_ge(qr_lo, 4)
                pe.wait_ge(prod_lo, PAIRS)
                for g in range(GROUPS):
                    for j in range(4):
                        if g == 0 and j == 0:
                            pe.wait_ge(k_lat, b + 1)
                            pe.wait_ge(k_step, b * 11 + 2)
                        if g == 0 and j == 2:
                            turn_values()
                        if g == 0 and j == 3:
                            pe.wait_ge(cq_lod, b * 4 + 4)
                        if g >= 1 and j < 2:
                            pe.wait_ge(rope_mul, b * 4 * GROUPS + 4 * g - 2 + 2 * j)
                        if g >= 1 and j >= 2:
                            pe.wait_ge(lat_out, b * 8 * GROUPS + 8 * g - 4 + 4 * (j - 2))
                        outs = ((Sa[:, 0:HALF], Sa[:, HALF:S]), (Sb[:, 0:HALF], Sb[:, HALF:S]),
                                (Ta[:, :], Tb[:, :]), (Oa[:, :], Ob[:, :]))[j]
                        t = 4 * g + j
                        terms = ((Wq_hi[:, t, 0, :], cq_hi), (Wq_hi[:, t, 0, :], cq_lo), (Wq_lo[:, t, 0, :], cq_hi),
                                 (Wq_hi[:, t, 1, :], cq_s), (Wq_lo[:, t, 1, :], cq_s))
                        for k, (w, c) in enumerate(terms):
                            if g == 0 and j == 0 and k == 0:
                                pe.wait_ge(cq_hid, b * 3 + 1)
                            if g == 0 and j == 0 and k == 1:
                                pe.wait_ge(cq_lod, b * 4 + 1)
                            if g == 0 and j == 0 and k == 3:
                                pe.wait_ge(cq_lod, b * 4 + 3)
                            for n in range(2):
                                last = mm(outs[n], w, c[:, n * HALF:(n + 1) * HALF], start=(k == 0), stop=(k == 4))
                        last.then_inc(q_ps, 1)

                def scores(tile, n, pair):
                    a, q = n // 4 % 2, (n // 8 * 4 + n % 4) * P
                    if n in (0, 4):
                        pe.wait_ge(q_split_lo, pair * 2 + a + 1)
                    pe.wait_ge(exp_done, tile + 1)
                    bank = SS[n % 2]
                    for k, (w, c) in enumerate(((Q_hi, K_hi), (Q_hi, K_lo), (Q_lo, K_hi))):
                        for m in range(2):
                            last = mm(bank[:, m * HALF:(m + 1) * HALF], w[:, a, q:q + P], c[:, m * HALF:(m + 1) * HALF],
                                      start=(k == 0), stop=(k == 2))
                    last.then_inc(scores_ready, 1)

                def transpose_probs(tile, n):
                    pe.wait_ge(exp_done, EXP0 + tile + 1)
                    for j in range(2):
                        pe.wait_ge(pt_lo, tile * 2 + j + 1)
                        for k in range(4):
                            last = nc.tensor.transpose(TS[j][:, k * P:(k + 1) * P],
                                                       probs[:, n % 2, (4 * j + k) * P:(4 * j + k + 1) * P], ident[:, :])
                        last.then_inc(pt_ps, 1)

                def values(group, h, k):
                    if k == 0:
                        pe.wait_ge(pt_lo, LO0 + group * 16 + 16)
                        pe.wait_ge(out_ready, group + 1)
                    for i, (v, pt) in enumerate(((V_hi, PT_hi), (V_lo, PT_hi), (V_hi, PT_lo))):
                        for a in range(2):
                            last = mm(Oa[64 * a:64 * a + 64, :], v[:, k, :], pt[:, 1 - h, a, k, :],
                                      start=(k == 0 and i == 0), stop=(k == KT - 1 and i == 2))
                    if k == KT - 1:
                        last.then_inc(pv_done, 1)

                def sums_to_rows(group):
                    pe.wait_ge(wide_ready, group + 1)
                    pe.wait_ge(row_ready, group + 1)
                    for t in range(4):
                        last = nc.tensor.transpose(Ob[:, t * P:(t + 1) * P], rden_wide[:, t], ident[:, :])
                    last.then_inc(row_ps, 1)

                def pair_pe(p, first, last):
                    pair = b * PAIRS + p
                    t0 = pair * TILES
                    for n in range(TILES):
                        if not (last and n >= TILES - 2):
                            scores(t0 + n + 2, (n + 2) % TILES, pair + (n + 2) // TILES)
                        transpose_probs(t0 + n, n)
                        if not (first and n < 8):
                            values(pair * 2 + n // 8 - 1, 1 - n // 8, n % 8)
                            if n % 8 == 2:
                                sums_to_rows(pair * 2 + n // 8 - 1)

                pe.wait_ge(k_step, b * 11 + 11)
                pe.wait_ge(rope_mul, b * 4 * GROUPS + 4 * GROUPS)
                for n in range(2):
                    scores(b * PAIRS * TILES + n, n, b * PAIRS)
                pe.wait_ge(lat_out, b * 8 * GROUPS + 8 * GROUPS)
                pair_pe(0, True, False)
                with pe.Fori(1, PAIRS - 1) as p:
                    pair_pe(p, False, False)
                pair_pe(PAIRS - 1, False, True)
                group = b * PAIRS * 2 + 2 * PAIRS - 1

                def project_out(t):
                    if t < 4:
                        pe.wait_ge(exp_done, EXP0 + b * TILES * PAIRS + TILES * PAIRS)
                    else:
                        pe.wait_ge(att_res, b * 48 + 3 * (t - 4) + 1)
                    for j in range(PAIRS):
                        if t in (0, 4) and j == PAIRS - 2:
                            pe.wait_ge(out_ready, OUT0 + b * 2 * PAIRS + 2 * PAIRS - 2 + t // 4)
                        if t in (0, 4) and j == PAIRS - 1:
                            pe.wait_ge(out_ready, OUT0 + b * 2 * PAIRS + 2 * PAIRS - 1 + t // 4)
                        last = mm(SQ[t % 4][:, 0:D], QO[:, 2 * j, t * P:(t + 1) * P], Wvo[:, j, :],
                                  start=(j == 0), stop=(j == PAIRS - 1))
                    last.then_inc(att_ps, 1)

                def turn_x1(h):
                    pe.wait_ge(x1_ready, b * 8 + 4 * h + 4)
                    if h:
                        pe.wait_ge(x1T_lod, b * 4 + 2)
                    else:
                        pe.wait_ge(pt_lo, LO0 + b * 2 * TILES * PAIRS + 2 * TILES * PAIRS)
                    for c in range(KC):
                        for t in range(4):
                            last = nc.tensor.transpose(TS[c][:, t * P:(t + 1) * P],
                                                       tok(x1, 4 * h + t)[:, c * P:(c + 1) * P], ident[:, :])
                    last.then_inc(x1T_ps, 1)

                def hidden(h, t):
                    u = b * 2 * HT + HT * h + t
                    if HT * h + t >= 2:
                        pe.wait_ge(gate_done, u - 1)
                    elif t == 0:
                        pe.wait_ge(row_ready, ROW0 + b * 2 * PAIRS + 2 * PAIRS)
                    else:
                        pe.wait_ge(att_res, b * 48 + 3 * 5 + 1)
                    banks = ((Oa[:, :], Ob[:, :]), SQ[0:2])[t % 2]
                    for i in range(2):
                        for k in range(4):
                            w = TT[:, (i * 2 * HT + k // 2 * HT + t) * P:(i * 2 * HT + k // 2 * HT + t + 1) * P]
                            last = mm(banks[i], w, (x1T_hi, x1T_lo)[k % 2][:, k // 2, :], start=(k == 0), stop=(k == 3))
                    last.then_inc(h_ps, 1)

                def down(h):
                    for t in range(4 * h, 4 * h + 4, 2):
                        for i in range(HT):
                            if t % 4 == 0:
                                pe.wait_ge(glo_done, b * 2 * HT + HT * h + i + 1)
                            w = TT[:, 4 * HT * P + i * D:4 * HT * P + (i + 1) * D]
                            for u in range(t, t + 2):
                                if i == 0:
                                    pe.wait_ge(att_res, b * 48 + (24 if u < 2 else 24 + 3 * (u - 2) + 1))
                                for k in range(2):
                                    last = mm(SQ[2 + u % 2][:, 0:D], (g_hi, g_lo)[k][:, i, u % 4 * P:u % 4 * P + P], w,
                                              start=(i == 0 and k == 0), stop=(i == HT - 1 and k == 1))
                                if i == HT - 1:
                                    last.then_inc(y_ps, 1)

                project_out(0)
                sums_to_rows(group)
                for t in range(1, 4):
                    project_out(t)
                for k in range(KT):
                    values(group, 1, k)
                turn_x1(0)
                for t in range(4, QT):
                    project_out(t)
                pe.wait_ge(tt_in, b * 16 + 16)
                for h in range(2):
                    pe.wait_ge(x1T_lod, b * 4 + 2 * h + 2)
                    for t in range(HT):
                        hidden(h, t)
                    if h == 0:
                        turn_x1(1)
                    down(h)


_INS = ['L0_attn_x', 'L0_attn_w_dkv', 'L0_attn_w_kr', 'L0_attn_w_uk', 'L0_attn_w_uv', 'L0_attn_w_dq',
        'L0_attn_w_qr', 'L0_attn_w_uq', 'L0_attn_w_o', 'L0_ffn_w1', 'L0_ffn_w3', 'L0_ffn_w2']


def kernel(**inputs):
    import concourse.bacc as _bacc
    from concourse.bass_utils import run_bass_kernel_spmd as _run

    nc = _bacc.Bacc("TRN2", target_bir_lowering=False, num_devices=1)
    arrays, args = {}, []
    cos, sin = rope_tables()
    given = [(f"in_{n}_dram", inputs[n]) for n in _INS] + [("rope_cos", cos), ("rope_sin", sin)]
    for name, a in given:
        a = np.ascontiguousarray(a)
        arrays[name] = a
        args.append(nc.dram_tensor(name, a.shape, mybir.dt.from_np(a.dtype), kind="ExternalInput").ap())
    args.append(nc.dram_tensor("out_dram", (B, S, D), mybir.dt.float32, kind="ExternalOutput").ap())
    build(nc, *args)
    r = _run(nc, [arrays], core_ids=[0])
    return r.results[0]["out_dram"]
```

```python
import math
from contextlib import ExitStack

import numpy as np

import concourse.bass as bass
from concourse import mybir

B, S, D = 2, 1024, 256
H, DR, DN, DV = 16, 64, 128, 128
KVR, QR = 64, 192
HID = 682
THETA = 10000.0
EPS = 1e-5
P = 128
QT = S // P
KT = S // P
KC = D // P
PAIRS = H // 2
HALF = S // 2
GROUPS = 4
HT = -(-HID // P)
LAST = HID - (HT - 1) * P
W = 3 * HT * D
PROB_UP = 2.0 ** 14
VAL_UP = 2.0 ** 8
TILES = 4 * 4

EXP0, PT0, LO0, PV0, OUT0, ROW0, Y0, STORED0, READ0 = 2, 4, 2, 1, 1, 1, 2, 1, 1


def rope_tables():
    inv = np.float32(1.0) / np.float32(THETA) ** (np.arange(0, DR, 2, dtype=np.float32) / np.float32(DR))
    ang = np.arange(S, dtype=np.float32)[:, None] * inv[None, :].astype(np.float32)
    cos = np.cos(ang.astype(np.float64)).astype(np.float32).T
    sin = np.sin(ang.astype(np.float64)).astype(np.float32).T
    return np.ascontiguousarray(np.tile(cos, (4, 1))), np.ascontiguousarray(np.tile(sin, (4, 1)))


def build(nc, x, w_dkv, w_kr, w_uk, w_uv, w_dq, w_qr, w_uq, w_o, w1, w3, w2, cos, sin, out):
    F = mybir.dt.float32
    R = mybir.dt.float32r
    F16 = mybir.dt.float16
    I32 = mybir.dt.int32
    ALU = mybir.AluOpType
    ACT = mybir.ActivationFunctionType
    AX = mybir.AxisListType
    SCALE = 1.0 / math.sqrt(DR + DN)

    x_v = x.rearrange("b (t p) d -> b p t d", p=P)
    out_v = out.rearrange("b (t p) d -> b p t d", p=P)
    wo_v = w_o.rearrange("(h n) d -> n h d", n=DV)
    ternary = nc.dram_tensor("ternary", [P, W], F, kind="Internal").ap()
    wvo_low = nc.dram_tensor("wvo_low", [P, PAIRS * D], F, kind="Internal").ap()

    ctx = ExitStack()
    with ctx:
        def sem(name):
            return ctx.enter_context(nc.semaphore(name))

        def sb(stack, name, shape, dt):
            return stack.enter_context(nc.sbuf_tensor(name, shape, dt))

        base = -(-nc.sbuf_base // 64) * 64
        arena = sb(ctx, "arena", [P, (nc.sbuf_usable_end - base) // 4 - 32], F)
        top = [0]

        def lay(start, *tensors):
            made, at = [], start
            for name, shape, dt in tensors:
                made.append(nc.alloc_sbuf_tensor_at(name, shape, dt, offset=base + at))
                at += -(-math.prod(shape[1:]) * (2 if dt == F16 else 4) // 64) * 64
            top[0] = max(top[0], at)
            return made, at

        (ident, Wq_hi, Wq_lo, Wvo_hi), K_AT = lay(
            0, ("ident", [P, P], F),
            ("Wq_hi", [P, H, 2, P], R), ("Wq_lo", [P, H, 2, P], R),
            ("Wvo_hi", [P, PAIRS, D], R))
        (K_hi, K_lo, V_hi, V_lo, vscale, ffs, minus_half, nmax, den, rden, rden_wide, rden_row, stats, mv, ve,
         rstd), QO_AT = lay(
            K_AT, ("K_hi", [P, S], R), ("K_lo", [P, S], R),
            ("V_hi", [P, KT, KVR], F16), ("V_lo", [P, KT, KVR], F16),
            ("vscale", [P, 4], F),
            ("ffs", [P, 8], F),
            ("minus_half", [P, 4], F),
            ("nmax", [P, 4], F), ("den", [P, 2, 2, 4], F), ("rden", [P, 2, 2, 4], F),
            ("rden_wide", [P, 4, 2, KVR], F),
            ("rden_row", [P, HALF], F),
            ("stats", [P, QT, 6], F), ("mv", [P, QT, 2], F), ("ve", [P, QT], F), ("rstd", [P, QT], F))
        (Wvo_lo,), _ = lay(K_AT, ("Wvo_lo", [P, PAIRS, D], R))
        (QO,), HEAD_AT = lay(QO_AT, ("QO", [P, H, S], F))
        (O_parts,), _ = lay(QO_AT, ("O_parts", [P, H, S], R))

        (Q_hi, Q_lo, probs), SHARED_AT = lay(
            HEAD_AT, ("Q_hi", [P, 2, S], R), ("Q_lo", [P, 2, S], R), ("probs", [P, 2, S], F))
        (TT,), _ = lay(HEAD_AT, ("TT", [P, W], R))
        (PT_hi, PT_lo), _ = lay(SHARED_AT, ("PT_hi", [P, 2, 2, KT, HALF], F16), ("PT_lo", [P, 2, 2, KT, HALF], F16))
        (xq, xT, tcos, tsin, wkr, wkv, wdq, wdq_b), WORK_AT = lay(
            SHARED_AT, ("xq", [P, QT, D], F), ("xT", [P, KC, S], F), ("tcos", [P, S], F), ("tsin", [P, S], F),
            ("wkr", [P, KC, DR], F), ("wkv", [P, KC, P], F), ("wdq", [P, KC, P], F),
            ("wdq_b", [P, KC, 2, QR - P], F))
        (cq_hi, cq_lo, cq_s), MUL_AT = lay(
            WORK_AT, ("cq_hi", [P, S], R), ("cq_lo", [P, S], R),
            ("cq_s", [P, S], R))
        (qmul,), _ = lay(MUL_AT, ("qmul", [P, 4, S], F))
        (Kf, kmul), _ = lay(MUL_AT, ("Kf", [P, S], F), ("kmul", [P, 2, S], F))
        (turned,), _ = lay(SHARED_AT, ("turned", [P, 2, S], F))
        PT_BYTES = KT * S * 2
        (res1,), AT = lay(WORK_AT, ("res1", [P, 4, D], F))
        assert AT <= SHARED_AT + 2 * PT_BYTES
        (xr, res0, x1a), _ = lay(
            SHARED_AT + 3 * PT_BYTES, ("xr", [P, QT, D], F), ("res0", [P, 4, D], F), ("x1a", [P, 4, D], F))
        (x1b, x1T_hi0, x1T_lo0), AT = lay(
            SHARED_AT + 2 * PT_BYTES, ("x1b", [P, 4, D], F), ("x1T_hi0", [P, KC, HALF], R),
            ("x1T_lo0", [P, KC, HALF], R))
        assert AT <= SHARED_AT + 3 * PT_BYTES

        def tok(halves, t):
            return halves[t // 4][:, t % 4, :]

        xr_h, res, x1 = (xr[:, 0:4, :], xr[:, 4:8, :]), (res0, res1), (x1a, x1b)
        act = QO[:, 0, :].rearrange("p (t q) -> p t q", t=2)
        gate = QO[:, 2, :].rearrange("p (t q) -> p t q", t=2)
        (x1T_hi1,), _ = lay(QO_AT + 4 * S, ("x1T_hi1", [P, KC, HALF], R))
        (x1T_lo1,), _ = lay(QO_AT + 3 * 4 * S, ("x1T_lo1", [P, KC, HALF], R))
        (g_hi, g_lo), AT = lay(QO_AT + 4 * 4 * S, ("g_hi", [P, HT, HALF], R), ("g_lo", [P, HT, HALF], R))
        assert AT <= QO_AT + 14 * 4 * S
        yo = tuple(QO[:, 14 + h, :].rearrange("p (t d) -> p t d", d=D) for h in range(2))
        x1T_hi, x1T_lo = (x1T_hi0, x1T_hi1), (x1T_lo0, x1T_lo1)
        (wuq_a, wuq_b, wuk, wuv, wo, wqr), AT = lay(
            QO_AT, ("wuq_a", [P, H * DN], F), ("wuq_b", [QR - P, H * DN], F), ("wuk", [KVR, H * DN], F),
            ("wuv", [KVR, H * DV], F), ("wo", [P, H, D], F), ("wqr", [P, 2, H * DR], F))
        (ones, asum), AT = lay(AT, ("ones", [P, P], F), ("asum", [P, 4], F))
        assert AT <= HEAD_AT
        (tern,), AT = lay(HEAD_AT, ("tern", [P, W], R))
        (below,), AT = lay(AT, ("below", [P, HT * D], F))
        assert AT <= SHARED_AT
        (w13, w2n, wT, AT_sb), _ = lay(
            WORK_AT, ("w13", [P, 2, HT, D], F), ("w2n", [P, KC, HT * P], F), ("wT", [P, 2, QR + 2 * KVR], F),
            ("AT", [P, 2, 2, P], F))
        ff = (w13[:, 0, :, :].rearrange("p t d -> p (t d)"), w13[:, 1, :, :].rearrange("p t d -> p (t d)"),
              w2n[:, :, :].rearrange("p t h -> p (t h)"))
        assert top[0] <= 4 * arena.shape[1], (top[0], 4 * arena.shape[1])

        Sa = ctx.enter_context(nc.psum_tensor("Sa", [P, S], F))
        Sb = ctx.enter_context(nc.psum_tensor("Sb", [P, S], F))
        Ta = ctx.enter_context(nc.psum_tensor("Ta", [P, HALF], F))
        Tb = ctx.enter_context(nc.psum_tensor("Tb", [P, HALF], F))
        Oa = ctx.enter_context(nc.psum_tensor("Oa", [P, HALF], F))
        Ob = ctx.enter_context(nc.psum_tensor("Ob", [P, HALF], F))
        SS, TS, OS = (Sa, Sb), (Ta, Tb), (Oa, Ob)
        SQ = (Sa[:, 0:HALF], Sa[:, HALF:S], Sb[:, 0:HALF], Sb[:, HALF:S])
        Y_BANKS = (SQ[2], SQ[3], SQ[2], SQ[3], SQ[2], SQ[3], Ta[:, :], Tb[:, :])
        FF = (SQ[2], SQ[3], Ta[:, :], Tb[:, :])

        held = sem("held")
        const_ready = sem("const_ready")
        w_qk_in = tuple(sem(f"w_qk_in{i}") for i in range(4))
        w_o_in = tuple(sem(f"w_o_in{i}") for i in range(4))
        w_uv_in = sem("w_uv_in")
        w_qr_in, w13_in, w2_in = sem("w_qr_in"), sem("w13_in"), sem("w2_in")
        pad_ready = sem("pad_ready")
        wt_ps, wt_sb = sem("wt_ps"), sem("wt_sb")
        prod_ps, at_sb, back_ps = sem("prod_ps"), sem("at_sb"), sem("back_ps")
        wvo_hid, wvo_sb, wvo_out = sem("wvo_hid"), sem("wvo_sb"), sem("wvo_out")
        prod_hi, prod_lo = sem("prod_hi"), sem("prod_lo")
        qr_hi, qr_lo = sem("qr_hi"), sem("qr_lo")
        ff_sum, abs_done, ff_mean, ff_step = sem("ff_sum"), sem("abs_done"), sem("ff_mean"), sem("ff_step")
        ff_tern, ff_ps, ff_sb, ff_out = sem("ff_tern"), sem("ff_ps"), sem("ff_sb"), sem("ff_out")
        proj_in = sem("proj_in")
        w_small = sem("w_small")
        xT_ps, xT_sb = sem("xT_ps"), sem("xT_sb")
        kv_ps, cqa_ps, cqb_ps = sem("kv_ps"), sem("cqa_ps"), sem("cqb_ps")
        k_lat, k_step, k_hi = sem("k_lat"), sem("k_step"), sem("k_hi")
        v_ps, v_hi = sem("v_ps"), sem("v_hi")
        cq_hid, cq_lod = sem("cq_hid"), sem("cq_lod")
        q_ps, rope_mul, rope_sum, lat_out = sem("q_ps"), sem("rope_mul"), sem("rope_sum"), sem("lat_out")
        turned_out = (sem("even_out"), sem("odd_out"))
        q_split_hi, q_split_lo = sem("q_split_hi"), sem("q_split_lo")
        scores_ready, max_ready, exp_done = sem("scores_ready"), sem("max_ready"), sem("exp_done")
        pt_ps, pt_hi, pt_lo = sem("pt_ps"), sem("pt_hi"), sem("pt_lo")
        pv_done, rden_ready, row_ps, row_ready = sem("pv_done"), sem("rden_ready"), sem("row_ps"), sem("row_ready")
        wide_ready = sem("wide_ready")
        out_ready, out_hi, out_lo = sem("out_ready"), sem("out_hi"), sem("out_lo")
        wvo_in = sem("wvo_in")
        xr_in, tt_in = sem("xr_in"), sem("tt_in")
        att_ps, att_res, ln_step, ln_pow = sem("att_ps"), sem("att_res"), sem("ln_step"), sem("ln_pow")
        x1_ready, x1T_ps, x1T_hid, x1T_lod = sem("x1_ready"), sem("x1T_ps"), sem("x1T_hid"), sem("x1T_lod")
        h_ps, silu_done, gate_done = sem("h_ps"), sem("silu_done"), sem("gate_done")
        ghi_done, glo_done, y_ps = sem("ghi_done"), sem("glo_done"), sem("y_ps")
        y_ready, y_out, y_stored = sem("y_ready"), sem("y_out"), sem("y_stored")
        y_read = sem("y_read")

        block = ctx.enter_context(nc.Block())

        def hold(eng, s, value):
            eng.wait_ge(s, value)
            eng.sem_inc(held, 1)

        @block.sync
        def _(sp):
            def absorbed_weights(part, heads):
                cols = slice(heads[0] * DN, heads[1] * DN)
                sp.dma_start(wuq_a[:, cols], w_uq[0:P, cols]).then_inc(w_qk_in[part], 16)
                sp.dma_start(wuq_b[:, cols], w_uq[P:QR, cols]).then_inc(w_qk_in[part], 16)
                if part:
                    sp.dma_start(wuk[:, cols], w_uk[:, cols]).then_inc(w_qk_in[part], 16)
                    sp.dma_start(wuv[:, cols], w_uv[:, cols]).then_inc(w_qk_in[part], 16)

            def output_weights(part):
                heads = slice(4 * part, 4 * part + 4)
                sp.dma_start(wo[:, heads, :], wo_v[:, heads, :]).then_inc(w_o_in[part], 16)

            absorbed_weights(0, (0, 4))
            output_weights(0)
            absorbed_weights(1, (4, 8))
            output_weights(1)
            sp.wait_ge(pad_ready, 3)
            for i, w in enumerate((w1, w3)):
                sp.dma_start(w13[:, i, 0:HT - 1, :],
                             w[0:(HT - 1) * P, :].rearrange("(t p) d -> p t d", p=P)).then_inc(w13_in, 16)
                sp.dma_start(w13[0:LAST, i, HT - 1, :], w[(HT - 1) * P:HID, :]).then_inc(w13_in, 16)
            absorbed_weights(2, (8, 12))
            output_weights(2)
            sp.dma_start(w2n[:, :, 0:HID], w2.rearrange("(t p) h -> p t h", p=P)).then_inc(w2_in, 16)
            absorbed_weights(3, (12, H))
            output_weights(3)
            sp.dma_start(wqr[:, 0, :], w_qr[0:P, :]).then_inc(w_qr_in, 16)
            sp.dma_start(wqr[0:64, 1, :], w_qr[P:QR, :]).then_inc(w_qr_in, 16)
            sp.dma_start(wqr[64:128, 1, :], w_qr[P:QR, :]).then_inc(w_qr_in, 16)

            with sp.Fori(0, B) as b:
                sp.wait_ge(pv_done, b * 2 * PAIRS + PV0)
                sp.dma_start(xq[:, :, :], x_v[b]).then_inc(proj_in, 16)
                for kc in range(KC):
                    rows = slice(kc * P, (kc + 1) * P)
                    sp.dma_start(wkr[:, kc, :], w_kr[rows, :]).then_inc(proj_in, 16)
                    sp.dma_start(wkv[:, kc, DR:P], w_dkv[rows, :]).then_inc(proj_in, 16)
                    sp.dma_start(wdq[:, kc, :], w_dq[rows, 0:P]).then_inc(proj_in, 16)
                    for a in range(2):
                        sp.dma_start(wdq_b[:, kc, a, :], w_dq[rows, P:QR]).then_inc(proj_in, 16)
                sp.dma_start(tcos[:, :], cos).then_inc(proj_in, 16)
                sp.dma_start(tsin[:, :], sin).then_inc(proj_in, 16)
                for g in range(GROUPS):
                    if g == 3:
                        hold(sp, y_stored, b + STORED0)
                    for j in range(2):
                        sp.wait_ge(rope_sum, b * 2 * GROUPS + 2 * g + j + 1)
                        for s in range(4):
                            sp.dma_start(QO[32 * j:32 * j + 32, 4 * g + s, :],
                                         turned[32 * s:32 * s + 32, j, :]).then_inc(turned_out[j], 16)
                hold(sp, scores_ready, b * TILES * PAIRS + TILES * PAIRS)
                sp.wait_ge(wvo_out, 16)
                sp.dma_start(Wvo_lo[:, :, :].rearrange("p j d -> p (j d)").bitcast(F), wvo_low).then_inc(wvo_in, 16)
                sp.wait_ge(pv_done, b * 2 * PAIRS + PV0 + 2 * PAIRS - 1)
                sp.dma_start(xr[:, :, :], x_v[b]).then_inc(xr_in, 16)
                sp.wait_ge(ff_out, 16)
                sp.wait_ge(pt_ps, b * 2 * TILES * PAIRS + 2 * TILES * PAIRS + PT0)
                sp.dma_start(TT[:, :].bitcast(F), ternary).then_inc(tt_in, 16)

        @block.gpsimd
        def _(pool):
            nc.gpsimd.memset(ident[:, :], 0.0).then_inc(const_ready, 1)
            nc.gpsimd.memset(ones[:, :], 1.0).then_inc(const_ready, 1)
            nc.gpsimd.memset(minus_half[:, :], -0.5).then_inc(const_ready, 1)
            pool.wait_ge(const_ready, 3)
            nc.gpsimd.affine_select(out=ident[:, :], in_=ident[:, :], compare_op=ALU.not_equal, fill=1.0, base=0,
                                    pattern=[[-1, P]], channel_multiplier=1).then_inc(const_ready, 1)
            for i in range(2):
                nc.gpsimd.memset(w13[:, i, HT - 1, :], 0.0).then_inc(pad_ready, 1)
            nc.gpsimd.memset(w2n[:, :, HID:HT * P], 0.0).then_inc(pad_ready, 1)
            pool.sem_inc(y_stored, STORED0)

            with pool.Fori(0, B) as b:
                def split_low(tile, pair, a):
                    pool.wait_ge(q_split_hi, pair * 2 + a + 1)
                    nc.gpsimd.tensor_tensor(Q_lo[:, a, :], QO[:, tile, :], Q_hi[:, a, :].bitcast(F),
                                            ALU.subtract).then_inc(q_split_lo, 1)

                for g in range(GROUPS):
                    for j, op in enumerate((ALU.subtract, ALU.add)):
                        pool.wait_ge(rope_mul, b * 4 * GROUPS + 4 * g + j + 3)
                        if g >= 1:
                            pool.wait_ge(turned_out[j], b * 64 * GROUPS + 64 * g)
                        nc.gpsimd.tensor_tensor(turned[:, j, :], qmul[:, 2 * j, :], qmul[:, 2 * j + 1, :],
                                                op).then_inc(rope_sum, 1)
                    if g == 1:
                        for a in range(2):
                            split_low(a, b * PAIRS, a)

                def widen(group, h):
                    hold(pool, rden_ready, group + 1)
                    src = rden[:, h].rearrange("p a t -> p t a").unsqueeze(3).broadcast_to([P, 4, 2, KVR])
                    nc.gpsimd.tensor_scalar(rden_wide[:, :, :, :], src, 1.0, 1.0, ALU.mult,
                                            ALU.mult).then_inc(wide_ready, 1)

                def split_out(group, pair_row, h, last):
                    cols = slice(h * HALF, (h + 1) * HALF)
                    hold(pool, out_ready, OUT0 + group + 1)
                    if last:
                        nc.gpsimd.tensor_scalar(O_parts[:, pair_row, cols], QO[:, pair_row + 1, cols], 1.0, 1.0,
                                                ALU.mult, ALU.mult).then_inc(out_hi, 1)
                    else:
                        nc.gpsimd.tensor_copy(O_parts[:, pair_row, cols], QO[:, pair_row + 1, cols]).then_inc(out_hi, 1)
                    hold(pool, out_hi, group + 1)
                    nc.gpsimd.tensor_tensor(O_parts[:, pair_row + 1, cols], QO[:, pair_row + 1, cols],
                                            O_parts[:, pair_row, cols].bitcast(F), ALU.subtract).then_inc(out_lo, 1)

                def pair_pool(p, first, last):
                    pair = b * PAIRS + p
                    if not first:
                        widen(pair * 2 - 1, 1)
                        split_out(pair * 2 - 2, p * 2 - 2, 0, False)
                    widen(pair * 2, 0)
                    if not first:
                        split_out(pair * 2 - 1, p * 2 - 2, 1, False)
                    if not last:
                        for a in range(2):
                            split_low(p * 2 + 2 + a, pair + 1, a)

                pair_pool(0, True, False)
                with pool.Fori(1, PAIRS - 1) as p:
                    pair_pool(p, False, False)
                pair_pool(PAIRS - 1, False, True)
                widen(b * PAIRS * 2 + 2 * PAIRS - 1, 1)

                def power(h, n):
                    pool.wait_ge(ln_step, n)
                    nc.gpsimd.tensor_tensor(rstd[:, 4 * h:4 * h + 4], ve[:, 4 * h:4 * h + 4], minus_half[:, :],
                                            ALU.pow).then_inc(ln_pow, 1)

                for h in range(2):
                    split_out(b * PAIRS * 2 + 2 * PAIRS - 2 + h, 2 * PAIRS - 2, h, True)
                    power(h, b * 4 + h + 1)
                def low_part(h, t):
                    pool.wait_ge(ghi_done, b * 2 * HT + HT * h + t + 1)
                    nc.gpsimd.tensor_tensor(g_lo[:, t, :], gate[:, t % 2, :], g_hi[:, t, :].bitcast(F),
                                            ALU.subtract).then_inc(glo_done, 1)

                def store(h):
                    pool.wait_ge(y_ready, b * 2 + h + 1 + Y0)
                    nc.gpsimd.dma_start(out_v[b][:, 4 * h:4 * h + 4, :], yo[h]).then_inc(y_out, 16)

                for t in range(HT):
                    low_part(0, t)
                low_part(1, 0)
                low_part(1, 1)
                power(0, b * 4 + 3)
                for t in range(2, HT):
                    low_part(1, t)
                store(0)
                power(1, b * 4 + 4)
                store(1)
                pool.wait_ge(y_out, b * 32 + 32)
                pool.sem_inc(y_stored, 1)

        @block.scalar
        def _(act_):
            def copy(o, i, scale=1.0):
                return nc.scalar.activation(o, i, ACT.Copy, scale=scale)

            act_.dma_start(wuk[:, 0:4 * DN], w_uk[:, 0:4 * DN]).then_inc(w_uv_in, 16)
            act_.dma_start(wuv[:, 0:4 * DV], w_uv[:, 0:4 * DV]).then_inc(w_uv_in, 16)
            act_.sem_inc(exp_done, EXP0)
            act_.sem_inc(row_ready, ROW0)

            def weights_out(h):
                act_.wait_ge(wt_ps, h + 1)
                if h >= 2:
                    act_.wait_ge(prod_ps, h - 1)
                copy(wT[:, h % 2, :], TS[h % 2][:, 0:QR + 2 * KVR]).then_inc(wt_sb, 1)

            def products_out(j):
                act_.wait_ge(prod_ps, 2 * j + 2)
                if j >= 2:
                    act_.wait_ge(back_ps, j - 1)
                bank = OS[j % 2]
                copy(AT_sb[:, j % 2, 0, :], bank[:, 0:P])
                copy(AT_sb[:, j % 2, 1, :].rearrange("p (c r) -> p c r", c=2),
                     bank[:, P:QR].unsqueeze(1).broadcast_to([P, 2, QR - P])).then_inc(at_sb, 1)

            def product_high(j):
                act_.wait_ge(back_ps, j + 1)
                tile = 4 * (j // 2) + 2 + j % 2
                copy(Wq_hi[:, tile, :, :], SQ[j % 2][:, 0:256].rearrange("p (c m) -> p c m", c=2)).then_inc(prod_hi, 1)

            def absolute_sum(i):
                act_.wait_ge(*((w13_in, 64) if i == 1 else (w2_in, 16)))
                act_.wait_ge(pad_ready, 3)
                if i == 2:
                    act_.wait_ge(abs_done, 1)
                nc.scalar.activation(below[:, :], ff[i], ACT.Abs, accum_out=asum[:, i:i + 1]).then_inc(abs_done, 1)

            def rotary_high(j, c):
                act_.wait_ge(w_qr_in, 48)
                src = wqr[:, c, :].rearrange("p (g m two) -> p two g m", two=2, m=P)[:, j]
                copy(Wq_hi[:, j::4, c, :], src).then_inc(qr_hi, 1)

            weights_out(0)
            weights_out(1)
            for h in range(H):
                if h % 2:
                    products_out(h // 2)
                elif h:
                    product_high(h // 2 - 1)
                if h in (6, 7):
                    absolute_sum(h - 5)
                if h + 2 < H:
                    weights_out(h + 2)
                if h >= 12:
                    rotary_high((h - 12) // 2, h % 2)
            product_high(PAIRS - 1)
            for n in range(9):
                act_.wait_ge(ff_ps, n + 1)
                copy(tern[:, n * HALF:(n + 1) * HALF], FF[n % 4]).then_inc(ff_sb, 1)
            act_.wait_ge(wvo_sb, PAIRS)
            act_.dma_start(wvo_low, Wvo_lo[:, :, :].rearrange("p j d -> p (j d)").bitcast(F)).then_inc(wvo_out, 16)
            act_.wait_ge(ff_sb, 9)
            act_.dma_start(ternary, tern[:, :].bitcast(F)).then_inc(ff_out, 16)

            with act_.Fori(0, B) as b:
                act_.wait_ge(proj_in, b * 208 + 208)
                copy(wkv[:, :, 0:DR].rearrange("p c (two i) -> p c two i", two=2),
                     wkr[:, :, :].rearrange("p c (i two) -> p c two i", two=2)).then_inc(w_small, 1)
                for n in range(4):
                    act_.wait_ge(xT_ps, b * 4 + n + 1)
                    copy(xT[:, n % 2, n // 2 * HALF:(n // 2 + 1) * HALF], (Oa[:, :], Ob[:, :], SQ[0], SQ[1])[n]).then_inc(xT_sb, 1)
                act_.wait_ge(kv_ps, b + 1)
                copy(Kf[64:128, :], Sa[64:128, :]).then_inc(k_lat, 1)
                act_.wait_ge(cqa_ps, b + 1)
                act_.wait_ge(y_ready, b * 2 + Y0)
                copy(cq_hi[:, :], Sb[:, :], SCALE).then_inc(cq_hid, 1)
                act_.wait_ge(cqb_ps, b + 1)
                for n in range(2):
                    copy(cq_s[:, n * HALF:(n + 1) * HALF], TS[n][:, :], SCALE).then_inc(cq_hid, 1)
                act_.wait_ge(k_lat, b + 1)
                act_.wait_ge(k_step, b * 11 + 4)
                act_.wait_ge(wvo_out, 16)
                copy(K_hi[:, :], Kf[:, :]).then_inc(k_hi, 1)
                act_.wait_ge(v_ps, b + 1)
                copy(V_hi[:, :, :], Oa[:, :].rearrange("p (k c) -> p k c", k=KT)).then_inc(v_hi, 1)
                def split_high(tile, pair, a, free):
                    if free is not None:
                        act_.wait_ge(scores_ready, free)
                    copy(Q_hi[:, a, :], QO[:, tile, :]).then_inc(q_split_hi, 1)

                def exponent(tile, n):
                    act_.wait_ge(max_ready, tile + 1)
                    act_.wait_ge(pt_ps, tile * 2 + 2)
                    nc.scalar.activation(probs[:, n % 2, :], SS[n % 2][:, :], ACT.Exp, bias=nmax[:, n % 4:n % 4 + 1],
                                         accum_out=den[:, n // 8 % 2, n // 4 % 2, n % 4:n % 4 + 1]).then_inc(exp_done, 1)

                for g in range(GROUPS):
                    if g == 3:
                        act_.wait_ge(y_stored, b + STORED0)
                    for i in range(2):
                        if g == GROUPS - 1 and i == 1:
                            exponent(b * PAIRS * TILES, 0)
                        act_.wait_ge(q_ps, b * 4 * GROUPS + 4 * g + 3 + i)
                        for n in range(2):
                            for a in range(2):
                                bank = (TS, OS)[i][n]
                                copy(QO[64:128, 4 * g + 2 * i + a, n * HALF:(n + 1) * HALF],
                                     bank[64 * a:64 * a + 64, :]).then_inc(lat_out, 1)
                    if g == 1:
                        act_.wait_ge(ff_out, 16)
                        act_.wait_ge(lat_out, b * 8 * GROUPS + 8)
                        for j in range(2):
                            act_.wait_ge(turned_out[j], b * 64 * GROUPS + 64)
                        for a in range(2):
                            split_high(a, b * PAIRS, a, None)

                def transposed_high(tile, n):
                    for j in range(2):
                        act_.wait_ge(pt_ps, PT0 + tile * 2 + j + 1)
                        dst = PT_hi[:, 1 - n // 8, n // 4 % 2, 4 * j:4 * j + 4, n % 4 * P:n % 4 * P + P]
                        copy(dst, TS[j][:, :].rearrange("p (k q) -> p k q", k=4), PROB_UP).then_inc(pt_hi, 1)

                def row_out(group):
                    act_.wait_ge(row_ps, group + 1)
                    act_.wait_ge(out_ready, group + 1)
                    copy(rden_row[:, :], Ob[:, :]).then_inc(row_ready, 1)

                def pair_act(p, first, last):
                    pair = b * PAIRS + p
                    t0 = pair * TILES
                    for n in range(TILES):
                        if not (last and n == TILES - 1):
                            exponent(t0 + n + 1, n + 1)
                        if first and n == 8:
                            act_.wait_ge(lat_out, b * 8 * GROUPS + 8 * GROUPS)
                            for j in range(2):
                                act_.wait_ge(turned_out[j], b * 64 * GROUPS + 64 * GROUPS)
                        transposed_high(t0 + n, n)
                        if n in (3, 11) and not (first and n == 3):
                            row_out(pair * 2 + (n // 8) - 1)
                        if n in (10, 14) and not last:
                            split_high(p * 2 + 2 + n // 12, pair + 1, n // 12, t0 + (12 if n == 10 else 16))

                pair_act(0, True, False)
                with act_.Fori(1, PAIRS - 1) as p:
                    pair_act(p, False, False)
                pair_act(PAIRS - 1, False, True)
                row_out(b * PAIRS * 2 + 2 * PAIRS - 1)

                def x1_high(h):
                    act_.wait_ge(x1T_ps, b * 2 + h + 1)
                    for c in range(KC):
                        copy(x1T_hi[h][:, c, :], TS[c][:, :]).then_inc(x1T_hid, 1)

                def silu(h, t):
                    u = b * 2 * HT + HT * h + t
                    act_.wait_ge(h_ps, u + 1)
                    if HT * h + t >= 2:
                        act_.wait_ge(gate_done, u - 1)
                    bank = (Oa[:, :], Sa[:, 0:HALF])[t % 2]
                    nc.scalar.activation(act[:, t % 2, :], bank, ACT.Silu, scale=ffs[:, 0:1]).then_inc(silu_done, 1)

                def gate_high(h, t):
                    act_.wait_ge(gate_done, b * 2 * HT + HT * h + t + 1)
                    if h == 1 and t == 0:
                        act_.wait_ge(y_ps, b * 8 + 4)
                    copy(g_hi[:, t, :], gate[:, t % 2, :]).then_inc(ghi_done, 1)

                x1_high(0)
                for t in range(HT):
                    silu(0, t)
                    gate_high(0, t)
                    if t == 2:
                        x1_high(1)
                silu(1, 0)
                silu(1, 1)
                gate_high(1, 0)
                gate_high(1, 1)
                for t in range(2, HT):
                    silu(1, t)
                    gate_high(1, t)

        @block.vector
        def _(dve):
            dve.sem_inc(pt_lo, LO0)
            dve.sem_inc(out_ready, OUT0)
            dve.sem_inc(y_ready, Y0)
            dve.sem_inc(y_read, READ0)

            def product_value(j):
                dve.wait_ge(at_sb, j + 1)
                nc.vector.tensor_copy(Wvo_hi[:, j, :], OS[j % 2][:, 256:512]).then_inc(wvo_hid, 1)

            def product_low(j):
                dve.wait_ge(prod_hi, j + 1)
                tile = 4 * (j // 2) + 2 + j % 2
                nc.vector.tensor_tensor(Wq_lo[:, tile, :, :], SQ[j % 2][:, 0:256].rearrange("p (c m) -> p c m", c=2),
                                        Wq_hi[:, tile, :, :].bitcast(F), ALU.subtract).then_inc(prod_lo, 1)
                dve.wait_ge(wvo_hid, j + 1)
                nc.vector.tensor_tensor(Wvo_lo[:, j, :], OS[j % 2][:, 256:512], Wvo_hi[:, j, :].bitcast(F),
                                        ALU.subtract).then_inc(wvo_sb, 1)

            def ternary_scales():
                dve.wait_ge(ff_mean, 1)
                nc.vector.tensor_scalar(ffs[:, 0:3], Sb[:, 0:3], 1.0 / (HID * D), None, ALU.mult).then_inc(ff_step, 1)
                dve.wait_ge(ff_step, 1)
                nc.vector.tensor_scalar(ffs[:, 3:6], ffs[:, 0:3], 0.5, None, ALU.mult).then_inc(ff_step, 1)
                nc.vector.tensor_tensor(ffs[:, 6:7], ffs[:, 1:2], ffs[:, 2:3], ALU.mult).then_inc(ff_step, 1)
                dve.wait_ge(ff_step, 3)

            def ternary_below(i):
                if i:
                    dve.wait_ge(ff_tern, i)
                nc.vector.tensor_scalar(below[:, :], ff[i], -1.0, ffs[:, 3 + i:4 + i], ALU.mult, ALU.is_gt).then_inc(ff_step, 1)

            def ternary_weight(i):
                dve.wait_ge(ff_step, 4 + i)
                nc.vector.scalar_tensor_tensor(ff[i], ff[i], ffs[:, 3 + i:4 + i], below[:, :], ALU.is_gt,
                                               ALU.subtract).then_inc(ff_tern, 1)

            for j in range(PAIRS):
                product_value(j)
                if 4 <= j < 7:
                    ternary_below(j - 4)
                product_low(j)
                if j == 2:
                    dve.wait_ge(w13_in, 64)
                    dve.wait_ge(pad_ready, 3)
                    nc.vector.tensor_reduce(asum[:, 0:1], ff[0], AX.X, ALU.add,
                                            apply_absolute_value=True).then_inc(ff_sum, 1)
                if j == 3:
                    ternary_scales()
                if 4 <= j < 7:
                    ternary_weight(j - 4)
            for j in range(2):
                for c in range(2):
                    dve.wait_ge(qr_hi, 2 * j + c + 1)
                    src = wqr[:, c, :].rearrange("p (g m two) -> p two g m", two=2, m=P)[:, j]
                    nc.vector.tensor_tensor(Wq_lo[:, j::4, c, :], src, Wq_hi[:, j::4, c, :].bitcast(F),
                                            ALU.subtract).then_inc(qr_lo, 1)

            with dve.Fori(0, B) as b:
                K0 = b * 11
                dve.wait_ge(y_ready, b * 2 + Y0)
                dve.wait_ge(kv_ps, b + 1)
                nc.vector.tensor_tensor(kmul[0:64, 0, :], Sa[0:64, :], tcos[0:64, :], ALU.mult)
                nc.vector.tensor_tensor(kmul[32:64, 1, :], Sa[0:32, :], tsin[0:32, :], ALU.mult).then_inc(k_step, 1)
                nc.vector.tensor_tensor(kmul[0:32, 1, :], Sa[32:64, :], tsin[32:64, :], ALU.mult).then_inc(k_step, 1)
                dve.wait_ge(k_step, K0 + 2)
                nc.vector.tensor_tensor(Kf[0:32, :], kmul[0:32, 0, :], kmul[0:32, 1, :], ALU.subtract).then_inc(k_step, 1)
                nc.vector.tensor_tensor(Kf[32:64, :], kmul[32:64, 0, :], kmul[32:64, 1, :], ALU.add).then_inc(k_step, 1)
                dve.wait_ge(cq_hid, b * 3 + 1)
                nc.vector.scalar_tensor_tensor(cq_lo[:, :], Sb[:, :], SCALE, cq_hi[:, :].bitcast(F), ALU.mult,
                                               ALU.subtract).then_inc(cq_lod, 1)
                dve.wait_ge(cq_hid, b * 3 + 3)
                for n in range(2):
                    low = cq_s[64:128, n * HALF:(n + 1) * HALF]
                    nc.vector.scalar_tensor_tensor(low, TS[n][64:128, :], SCALE, low.bitcast(F), ALU.mult,
                                                   ALU.subtract).then_inc(cq_lod, 1)
                dve.wait_ge(k_lat, b + 1)
                nc.vector.tensor_reduce(vscale[64:128, 0:1], Kf[64:128, :], AX.X, ALU.max,
                                        apply_absolute_value=True).then_inc(k_step, 1)
                dve.wait_ge(k_step, K0 + 5)
                nc.vector.tensor_scalar(vscale[64:128, 1:2], vscale[64:128, 0:1], 1e-30, None, ALU.max).then_inc(k_step, 1)
                dve.wait_ge(k_step, K0 + 6)
                nc.vector.tensor_scalar(vscale[64:128, 0:1].bitcast(I32), vscale[64:128, 1:2].bitcast(I32),
                                        0x7F800000, None, ALU.bitwise_and).then_inc(k_step, 1)
                dve.wait_ge(k_step, K0 + 7)
                nc.vector.reciprocal(vscale[64:128, 2:3], vscale[64:128, 0:1]).then_inc(k_step, 1)
                nc.vector.tensor_scalar(vscale[64:128, 3:4], vscale[64:128, 0:1], 1.0 / (PROB_UP * VAL_UP), None,
                                        ALU.mult).then_inc(k_step, 1)
                dve.wait_ge(k_step, K0 + 9)
                nc.vector.tensor_copy(vscale[0:64, 3:4], vscale[64:128, 3:4])
                nc.vector.tensor_scalar(kmul[64:128, 0, :], Kf[64:128, :], vscale[64:128, 2:3], VAL_UP, ALU.mult,
                                        ALU.mult).then_inc(k_step, 1)
                dve.wait_ge(k_hi, b + 1)
                nc.vector.tensor_tensor(K_lo[:, :], Kf[:, :], K_hi[:, :].bitcast(F), ALU.subtract).then_inc(k_step, 1)
                dve.wait_ge(v_hi, b + 1)
                nc.vector.tensor_tensor(V_lo[:, :, :], Oa[:, :].rearrange("p (k c) -> p k c", k=KT), V_hi[:, :, :],
                                        ALU.subtract).then_inc(cq_lod, 1)
                dve.wait_ge(k_step, K0 + 11)
                for g in range(GROUPS):
                    for j, (tile, table, dst) in enumerate(((0, tcos, 0), (0, tsin, 2), (1, tsin, 1), (1, tcos, 3))):
                        if tile == j // 2 and j % 2 == 0:
                            dve.wait_ge(q_ps, b * 4 * GROUPS + 4 * g + tile + 1)
                        if g >= 1:
                            dve.wait_ge(rope_sum, b * 2 * GROUPS + 2 * g - 1 + dst // 2)
                        nc.vector.tensor_tensor(qmul[:, dst, :], SS[tile][:, :], table[:, :], ALU.mult).then_inc(rope_mul, 1)

                def maximum(tile, n):
                    dve.wait_ge(scores_ready, tile + 1)
                    nc.vector.tensor_reduce(nmax[:, n % 4:n % 4 + 1], SS[n % 2][:, :], AX.X, ALU.max,
                                            negate=True).then_inc(max_ready, 1)

                def transposed_low(tile, n):
                    for j in range(2):
                        dve.wait_ge(pt_hi, tile * 2 + j + 1)
                        place = (slice(None), 1 - n // 8, n // 4 % 2, slice(4 * j, 4 * j + 4), slice(n % 4 * P, n % 4 * P + P))
                        nc.vector.scalar_tensor_tensor(PT_lo[place], TS[j][:, :].rearrange("p (k q) -> p k q", k=4),
                                                       PROB_UP, PT_hi[place], ALU.mult, ALU.subtract).then_inc(pt_lo, 1)

                def reciprocal(group, h):
                    dve.wait_ge(exp_done, EXP0 + group * 8 + 8)
                    nc.vector.reciprocal(rden[:, h], den[:, h]).then_inc(rden_ready, 1)

                def normalise(group, pair_row, h):
                    dve.wait_ge(pv_done, PV0 + group + 1)
                    dve.wait_ge(row_ready, ROW0 + group + 1)
                    nc.vector.scalar_tensor_tensor(QO[:, pair_row + 1, h * HALF:(h + 1) * HALF], Oa[:, :], vscale[:, 3:4],
                                                   rden_row[:, :], ALU.mult, ALU.mult).then_inc(out_ready, 1)

                def pair_dve(p, first, last):
                    pair = b * PAIRS + p
                    t0 = pair * TILES
                    for n in range(TILES):
                        h = n // 8
                        if n % 8 == 0:
                            if not first:
                                normalise(pair * 2 + h - 2, p * 2 - 2, h)
                            if not (first and h == 0):
                                reciprocal(pair * 2 + h - 1, 1 - h)
                        if not (last and n >= TILES - 2):
                            maximum(t0 + n + 2, n + 2)
                        transposed_low(t0 + n, n)

                for n in range(2):
                    maximum(b * PAIRS * TILES + n, n)
                dve.wait_ge(rope_sum, b * 2 * GROUPS + 2 * GROUPS)
                pair_dve(0, True, False)
                with dve.Fori(1, PAIRS - 1) as p:
                    pair_dve(p, False, False)
                pair_dve(PAIRS - 1, False, True)
                group = b * PAIRS * 2 + 2 * PAIRS
                normalise(group - 2, 2 * PAIRS - 2, 0)
                reciprocal(group - 1, 1)

                def statistics(t, n):
                    nc.vector.bn_stats(stats[:, t, :], tok(res, t)).then_inc(att_res, 1)
                    hold(dve, att_res, n + 2)
                    nc.vector.bn_aggr(mv[:, t, :], stats[:, t, :]).then_inc(att_res, 1)

                def add_eps(h, n):
                    dve.wait_ge(att_res, n)
                    nc.vector.tensor_scalar(ve[:, 4 * h:4 * h + 4], mv[:, 4 * h:4 * h + 4, 1], EPS, None,
                                            ALU.add).then_inc(ln_step, 1)

                A0 = b * 48

                def attention_rows(h):
                    for t in range(4 * h, 4 * h + 4):
                        dve.wait_ge(att_ps, b * 8 + t + 1)
                        nc.vector.tensor_tensor(tok(res, t), SQ[t % 4][:, 0:D], tok(xr_h, t), ALU.add).then_inc(att_res, 1)
                        dve.wait_ge(att_res, A0 + 3 * t + 1)
                        statistics(t, A0 + 3 * t)
                    add_eps(h, A0 + 12 * h + 12)

                def first_norm(h):
                    dve.wait_ge(ln_pow, b * 4 + h + 1)
                    for t in range(4 * h, 4 * h + 4):
                        nc.vector.tensor_scalar(tok(x1, t), tok(res, t), mv[:, t, 0:1], rstd[:, t:t + 1],
                                                ALU.subtract, ALU.mult).then_inc(x1_ready, 1)

                dve.wait_ge(xr_in, b * 16 + 16)
                attention_rows(0)
                first_norm(0)
                normalise(group - 1, 2 * PAIRS - 2, 1)

                def x1_low(h):
                    for c in range(KC):
                        dve.wait_ge(x1T_hid, b * 4 + 2 * h + c + 1)
                        nc.vector.tensor_tensor(x1T_lo[h][:, c, :], TS[c][:, :], x1T_hi[h][:, c, :].bitcast(F),
                                                ALU.subtract).then_inc(x1T_lod, 1)

                def gate_tile(h, t):
                    u = b * 2 * HT + HT * h + t
                    dve.wait_ge(silu_done, u + 1)
                    if HT * h + t >= 2:
                        dve.wait_ge(glo_done, u - 1)
                    bank = (Ob[:, :], Sa[:, HALF:S])[t % 2]
                    nc.vector.tensor_tensor(gate[:, t % 2, :], bank, act[:, t % 2, :], ALU.mult).then_inc(gate_done, 1)

                def result_row(t):
                    dve.wait_ge(y_ps, b * 8 + t + 1)
                    nc.vector.scalar_tensor_tensor(tok(res, t), Y_BANKS[t][:, 0:D], ffs[:, 6:7],
                                                   tok(x1, t), ALU.mult, ALU.add).then_inc(att_res, 1)

                def result_rows_0():
                    for t in range(4):
                        n = A0 + 24 + 3 * t
                        result_row(t)
                        dve.wait_ge(att_res, n + 1)
                        statistics(t, n)
                    add_eps(0, A0 + 36)

                def result_rows_1():
                    for t in range(4, 8):
                        result_row(t)
                    for t in range(4, 8):
                        dve.wait_ge(att_res, A0 + 36 + t - 3)
                        nc.vector.bn_stats(stats[:, t, :], tok(res, t)).then_inc(att_res, 1)
                    for t in range(4, 8):
                        hold(dve, att_res, A0 + 40 + t - 3)
                        nc.vector.bn_aggr(mv[:, t, :], stats[:, t, :]).then_inc(att_res, 1)
                    add_eps(1, A0 + 48)

                def second_norm(h):
                    dve.wait_ge(ln_pow, b * 4 + 3 + h)
                    for t in range(4 * h, 4 * h + 4):
                        last = nc.vector.tensor_scalar(tok(yo, t), tok(res, t), mv[:, t, 0:1], rstd[:, t:t + 1],
                                                       ALU.subtract, ALU.mult)
                    last.then_inc(y_ready, 1)

                x1_low(0)
                attention_rows(1)
                gate_tile(0, 0)
                first_norm(1)
                gate_tile(0, 1)
                gate_tile(0, 2)
                x1_low(1)
                for t in range(3, HT):
                    gate_tile(0, t)
                gate_tile(1, 0)
                gate_tile(1, 1)
                result_rows_0()
                gate_tile(1, 2)
                gate_tile(1, 3)
                second_norm(0)
                for t in range(4, HT):
                    gate_tile(1, t)
                result_rows_1()
                dve.sem_inc(y_read, 1)
                second_norm(1)

        @block.tensor
        def _(pe):
            mm = nc.tensor.matmul
            pe.sem_inc(pt_ps, PT0)
            pe.sem_inc(pv_done, PV0)

            pe.wait_ge(const_ready, 4)

            def turn_weights(h):
                if h % 4 == 0:
                    pe.wait_ge(w_qk_in[h // 4], 64 if h else 32)
                if h == 0:
                    pe.wait_ge(w_uv_in, 32)
                if h >= 2:
                    pe.wait_ge(wt_sb, h - 1)
                bank, cols = TS[h % 2], slice(h * DN, (h + 1) * DN)
                nc.tensor.transpose(bank[:, 0:128], wuq_a[:, cols], ident[:, :])
                nc.tensor.transpose(bank[:, 128:192], wuq_b[:, cols], ident[0:64, 0:64])
                nc.tensor.transpose(bank[:, 192:256], wuk[:, cols], ident[0:64, 0:64])
                nc.tensor.transpose(bank[:, 256:320], wuv[:, cols], ident[0:64, 0:64]).then_inc(wt_ps, 1)

            def weight_products(h):
                if h % 4 == 0:
                    pe.wait_ge(w_o_in[h // 4], 16)
                pe.wait_ge(wt_sb, h + 1)
                j, a = h // 2, h % 2
                if a == 0 and j >= 2:
                    pe.wait_ge(at_sb, j - 1)
                    pe.wait_ge(wvo_sb, j - 1)
                w, bank = wT[:, a, :], OS[j % 2]
                mm(bank[64 * a:64 * a + 64, 0:QR], w[:, 192:256], w[:, 0:QR], start=True, stop=True)
                mm(bank[64 * a:64 * a + 64, 256:512], w[:, 256:320], wo[:, h, :], start=True, stop=True).then_inc(prod_ps, 1)

            def turn_products(j):
                pe.wait_ge(at_sb, j + 1)
                if j >= 2:
                    pe.wait_ge(prod_lo, j - 1)
                nc.tensor.transpose(SQ[j % 2][:, 0:P], AT_sb[:, j % 2, 0, :], ident[:, :])
                nc.tensor.transpose(SQ[j % 2][:, P:2 * P], AT_sb[:, j % 2, 1, :], ident[:, :]).then_inc(back_ps, 1)

            def turn_ternary(n):
                pe.wait_ge(ff_tern, n // 3 + 1)
                if n >= 4:
                    pe.wait_ge(ff_sb, n - 3)
                for k in range(4):
                    i = 4 * (n % 3) + k
                    if n < 6:
                        src = w13[:, n // 3, i % HT, i // HT * P:i // HT * P + P]
                    else:
                        src = w2n[:, i % KC, i // KC * P:i // KC * P + P]
                    last = nc.tensor.transpose(FF[n % 4][:, k * P:(k + 1) * P], src, ident[:, :])
                last.then_inc(ff_ps, 1)

            turn_weights(0)
            turn_weights(1)
            for h in range(H):
                weight_products(h)
                if h == 8:
                    pe.wait_ge(ff_sum, 1)
                    pe.wait_ge(abs_done, 2)
                    mm(Sb[:, 0:3], ones[:, :], asum[:, 0:3], start=True, stop=True).then_inc(ff_mean, 1)
                if h % 2 == 0 and h:
                    turn_products(h // 2 - 1)
                if h + 2 < H:
                    turn_weights(h + 2)
                if h >= 14:
                    turn_ternary(h - 14)
            turn_products(PAIRS - 1)
            for n in range(2, 9):
                turn_ternary(n)
            pe.wait_ge(ff_sb, 8)
            pe.wait_ge(wvo_sb, PAIRS)
            pe.wait_ge(prod_lo, PAIRS)

            with pe.Fori(0, B) as b:
                pe.wait_ge(proj_in, b * 208 + 208)
                for n in range(4):
                    for t in range(4):
                        last = nc.tensor.transpose((Oa[:, :], Ob[:, :], SQ[0], SQ[1])[n][:, t * P:(t + 1) * P],
                                                   xq[:, n // 2 * 4 + t, n % 2 * P:n % 2 * P + P], ident[:, :])
                    last.then_inc(xT_ps, 1)
                pe.wait_ge(w_small, b + 1)

                def project(outs, lhs, signal):
                    for n in range(2):
                        if signal is kv_ps:
                            pe.wait_ge(xT_sb, b * 4 + n + 3)
                        for kc in range(KC):
                            last = mm(outs[n], lhs(kc), xT[:, kc, n * HALF:(n + 1) * HALF],
                                      start=(kc == 0), stop=(kc == KC - 1))
                    last.then_inc(signal, 1)

                project((Sa[:, 0:HALF], Sa[:, HALF:S]), lambda kc: wkv[:, kc, :], kv_ps)
                pe.wait_ge(ff_sb, 9)
                pe.wait_ge(y_read, b + READ0)
                project((Sb[:, 0:HALF], Sb[:, HALF:S]), lambda kc: wdq[:, kc, :], cqa_ps)
                project((Ta[:, :], Tb[:, :]), lambda kc: wdq_b[:, kc, :, :], cqb_ps)

                def turn_values():
                    hold(pe, k_step, b * 11 + 10)
                    for k in range(KT):
                        last = nc.tensor.transpose(Oa[:, k * KVR:(k + 1) * KVR], kmul[64:128, 0, k * P:(k + 1) * P],
                                                   ident[64:128, 64:128])
                    last.then_inc(v_ps, 1)

                pe.wait_ge(qr_lo, 4)
                def scores(tile, n, pair):
                    a, q = n // 4 % 2, (n // 8 * 4 + n % 4) * P
                    if n in (0, 4):
                        pe.wait_ge(q_split_lo, pair * 2 + a + 1)
                    pe.wait_ge(exp_done, tile + 1)
                    bank = SS[n % 2]
                    for k, (w, c) in enumerate(((Q_hi, K_hi), (Q_hi, K_lo), (Q_lo, K_hi))):
                        for m in range(2):
                            last = mm(bank[:, m * HALF:(m + 1) * HALF], w[:, a, q:q + P], c[:, m * HALF:(m + 1) * HALF],
                                      start=(k == 0), stop=(k == 2))
                    last.then_inc(scores_ready, 1)

                def transpose_probs(tile, n, waited):
                    if not waited:
                        pe.wait_ge(exp_done, EXP0 + tile + 1)
                    for j in range(2):
                        pe.wait_ge(pt_lo, tile * 2 + j + 1)
                        for k in range(4):
                            last = nc.tensor.transpose(TS[j][:, k * P:(k + 1) * P],
                                                       probs[:, n % 2, (4 * j + k) * P:(4 * j + k + 1) * P], ident[:, :])
                        last.then_inc(pt_ps, 1)

                def values(group, h, k):
                    if k == 0:
                        pe.wait_ge(pt_lo, LO0 + group * 16 + 16)
                        pe.wait_ge(out_ready, group + 1)
                    for i, (v, pt) in enumerate(((V_hi, PT_hi), (V_lo, PT_hi), (V_hi, PT_lo))):
                        for a in range(2):
                            last = mm(Oa[64 * a:64 * a + 64, :], v[:, k, :], pt[:, 1 - h, a, k, :],
                                      start=(k == 0 and i == 0), stop=(k == KT - 1 and i == 2))
                    if k == KT - 1:
                        last.then_inc(pv_done, 1)

                def sums_to_rows(group):
                    pe.wait_ge(wide_ready, group + 1)
                    pe.wait_ge(row_ready, group + 1)
                    for t in range(4):
                        last = nc.tensor.transpose(Ob[:, t * P:(t + 1) * P], rden_wide[:, t], ident[:, :])
                    last.then_inc(row_ps, 1)

                Q_BANKS = ((Sa[:, 0:HALF], Sa[:, HALF:S]), (Sb[:, 0:HALF], Sb[:, HALF:S]),
                           (Ta[:, :], Tb[:, :]), (Oa[:, :], Ob[:, :]))

                def query_terms(g, j, ks):
                    t = 4 * g + j
                    terms = ((Wq_hi[:, t, 0, :], cq_hi), (Wq_hi[:, t, 0, :], cq_lo), (Wq_lo[:, t, 0, :], cq_hi),
                             (Wq_hi[:, t, 1, :], cq_s), (Wq_lo[:, t, 1, :], cq_s))
                    for k in ks:
                        w, c = terms[k]
                        for n in range(2):
                            last = mm(Q_BANKS[j][n], w, c[:, n * HALF:(n + 1) * HALF], start=(k == 0), stop=(k == 4))
                    if 4 in ks:
                        last.then_inc(q_ps, 1)

                pe.wait_ge(k_lat, b + 1)
                pe.wait_ge(k_step, b * 11 + 2)
                pe.wait_ge(cq_hid, b * 3 + 1)
                query_terms(0, 0, (0,))
                pe.wait_ge(cq_lod, b * 4 + 1)
                query_terms(0, 0, (1, 2))
                query_terms(0, 1, (0, 1, 2))
                pe.wait_ge(cq_lod, b * 4 + 3)
                query_terms(0, 0, (3, 4))
                query_terms(0, 1, (3, 4))
                query_terms(0, 2, range(3))
                turn_values()
                query_terms(0, 2, (3, 4))
                pe.wait_ge(cq_lod, b * 4 + 4)
                query_terms(0, 3, range(5))
                for g in range(1, GROUPS):
                    for j in range(4):
                        if j < 2:
                            pe.wait_ge(rope_mul, b * 4 * GROUPS + 4 * g - 2 + 2 * j)
                        else:
                            pe.wait_ge(lat_out, b * 8 * GROUPS + 8 * g - 4 + 4 * (j - 2))
                        if g == GROUPS - 1 and j == 3:
                            pe.wait_ge(k_step, b * 11 + 11)
                            pe.wait_ge(rope_mul, b * 4 * GROUPS + 4 * GROUPS - 2)
                            scores(b * PAIRS * TILES, 0, b * PAIRS)
                        query_terms(g, j, range(5))

                def pair_pe(p, first, last):
                    pair = b * PAIRS + p
                    t0 = pair * TILES
                    for n in range(TILES):
                        if not (last and n >= TILES - 2):
                            scores(t0 + n + 2, (n + 2) % TILES, pair + (n + 2) // TILES)
                        transpose_probs(t0 + n, n, not (last and n >= TILES - 2))
                        if first and n == 8:
                            pe.wait_ge(lat_out, b * 8 * GROUPS + 8 * GROUPS)
                        if not (first and n < 8):
                            values(pair * 2 + n // 8 - 1, 1 - n // 8, n % 8)
                            if n % 8 == 2:
                                sums_to_rows(pair * 2 + n // 8 - 1)

                pe.wait_ge(rope_mul, b * 4 * GROUPS + 4 * GROUPS)
                scores(b * PAIRS * TILES + 1, 1, b * PAIRS)
                pe.wait_ge(lat_out, b * 8 * GROUPS + 8 * GROUPS - 4)
                pair_pe(0, True, False)
                with pe.Fori(1, PAIRS - 1) as p:
                    pair_pe(p, False, False)
                pair_pe(PAIRS - 1, False, True)
                group = b * PAIRS * 2 + 2 * PAIRS - 1

                def project_out(tiles):
                    h = tiles[0] // 4
                    for js in (range(PAIRS - 1), (PAIRS - 1,)):
                        pe.wait_ge(out_lo, b * 2 * PAIRS + (2 * PAIRS - 2 if js[0] == 0 else 2 * PAIRS - 1 + h))
                        for t in tiles:
                            if js[0] == 0:
                                if t < 4:
                                    pe.wait_ge(exp_done, EXP0 + b * TILES * PAIRS + TILES * PAIRS)
                                else:
                                    pe.wait_ge(att_res, b * 48 + 3 * (t - 4) + 1)
                            terms = [(O_parts[:, 2 * j + lo, t * P:(t + 1) * P], Wvo_hi[:, j, :])
                                     for j in js for lo in range(2)]
                            terms += [(O_parts[:, 2 * j, t * P:(t + 1) * P], Wvo_lo[:, j, :]) for j in js]
                            for k, (o, w) in enumerate(terms):
                                if t == 0 and k == 2 * (PAIRS - 1):
                                    pe.wait_ge(wvo_in, b * 16 + 16)
                                last = mm(SQ[t % 4][:, 0:D], o, w, start=(js[0] == 0 and k == 0),
                                          stop=(js[0] > 0 and k == len(terms) - 1))
                            if js[0] > 0:
                                last.then_inc(att_ps, 1)

                def turn_x1(h):
                    pe.wait_ge(x1_ready, b * 8 + 4 * h + 4)
                    if h:
                        pe.wait_ge(x1T_lod, b * 4 + 2)
                    else:
                        pe.wait_ge(pt_lo, LO0 + b * 2 * TILES * PAIRS + 2 * TILES * PAIRS)
                    for c in range(KC):
                        for t in range(4):
                            last = nc.tensor.transpose(TS[c][:, t * P:(t + 1) * P],
                                                       tok(x1, 4 * h + t)[:, c * P:(c + 1) * P], ident[:, :])
                    last.then_inc(x1T_ps, 1)

                def hidden(h, t):
                    u = b * 2 * HT + HT * h + t
                    if HT * h + t >= 2:
                        pe.wait_ge(gate_done, u - 1)
                    elif t == 0:
                        pe.wait_ge(row_ready, ROW0 + b * 2 * PAIRS + 2 * PAIRS)
                    else:
                        pe.wait_ge(att_res, b * 48 + 3 * 5 + 1)
                    banks = ((Oa[:, :], Ob[:, :]), SQ[0:2])[t % 2]
                    for i in range(2):
                        for k in range(4):
                            w = TT[:, (i * 2 * HT + k // 2 * HT + t) * P:(i * 2 * HT + k // 2 * HT + t + 1) * P]
                            last = mm(banks[i], w, (x1T_hi, x1T_lo)[k % 2][h][:, k // 2, :], start=(k == 0), stop=(k == 3))
                    last.then_inc(h_ps, 1)

                def down(tiles, hidden_tiles, waits):
                    for i in hidden_tiles:
                        if waits:
                            pe.wait_ge(glo_done, b * 2 * HT + HT * (tiles[0] // 4) + i + 1)
                        w = TT[:, 4 * HT * P + i * D:4 * HT * P + (i + 1) * D]
                        for u in tiles:
                            if i == 0 and u < 6:
                                pe.wait_ge(att_res, b * 48 + (24 if u < 2 else 24 + 3 * (u - 2) + 1))
                            for k in range(2):
                                last = mm(Y_BANKS[u][:, 0:D], (g_hi, g_lo)[k][:, i, u % 4 * P:u % 4 * P + P], w,
                                          start=(i == 0 and k == 0), stop=(i == HT - 1 and k == 1))
                            if i == HT - 1:
                                last.then_inc(y_ps, 1)

                project_out((0, 1))
                sums_to_rows(group)
                project_out((2, 3))
                for k in range(KT):
                    values(group, 1, k)
                turn_x1(0)
                project_out((4, 5))
                project_out((6, 7))
                pe.wait_ge(tt_in, b * 16 + 16)
                pe.wait_ge(x1T_lod, b * 4 + 2)
                hidden(0, 0)
                hidden(0, 1)
                hidden(0, 2)
                turn_x1(1)
                for t in range(3, HT):
                    hidden(0, t)
                pe.wait_ge(x1T_lod, b * 4 + 4)
                hidden(1, 0)
                down((0, 1), range(4), True)
                hidden(1, 1)
                down((0, 1), range(4, HT), True)
                down((2, 3), range(HT), False)
                for t in range(2, HT):
                    hidden(1, t)
                down((4, 5, 6, 7), range(HT), True)


_INS = ['L0_attn_x', 'L0_attn_w_dkv', 'L0_attn_w_kr', 'L0_attn_w_uk', 'L0_attn_w_uv', 'L0_attn_w_dq',
        'L0_attn_w_qr', 'L0_attn_w_uq', 'L0_attn_w_o', 'L0_ffn_w1', 'L0_ffn_w3', 'L0_ffn_w2']


def kernel(**inputs):
    import concourse.bacc as _bacc
    from concourse.bass_utils import run_bass_kernel_spmd as _run

    nc = _bacc.Bacc("TRN2", target_bir_lowering=False, num_devices=1)
    arrays, args = {}, []
    cos, sin = rope_tables()
    given = [(f"in_{n}_dram", inputs[n]) for n in _INS] + [("rope_cos", cos), ("rope_sin", sin)]
    for name, a in given:
        a = np.ascontiguousarray(a)
        arrays[name] = a
        args.append(nc.dram_tensor(name, a.shape, mybir.dt.from_np(a.dtype), kind="ExternalInput").ap())
    args.append(nc.dram_tensor("out_dram", (B, S, D), mybir.dt.float32, kind="ExternalOutput").ap())
    build(nc, *args)
    r = _run(nc, [arrays], core_ids=[0])
    return r.results[0]["out_dram"]
```
